# Optimizing a Trainium2 kernel written in Bass

```python
import numpy as np
import jax
import jax.numpy as jnp

def _softmax(x, axis=-1):
    return jax.nn.softmax(x, axis=axis)

def _gelu(x):
    return jax.nn.gelu(x, approximate=True)

def _silu(x):
    return jax.nn.silu(x)

def _sigmoid(x):
    return jax.nn.sigmoid(x)

def _layernorm(x, axis=-1, eps=1e-05):
    m = jnp.mean(x, axis=axis, keepdims=True)
    v = jnp.var(x, axis=axis, keepdims=True)
    return (x - m) / jnp.sqrt(v + eps)

def _scatter_add(tgt, idx, src, axis=0):
    return tgt.at[idx].add(src)

def _segment_sum(src, seg, n):
    return jax.ops.segment_sum(src, seg, n)
kernel_name = 'mk_gnn_preln_d2_gnn_r8_4f386d'

def setup_inputs(seed: int=0):
    np.random.seed(seed)
    _w = jnp.asarray

    def _rec_inputs():
        import jax
        import jax.numpy as jnp
        _gk = jax.random.key(seed)
        x = -0.0005121 + 1.001 * jax.random.normal(jax.random.fold_in(_gk, 1), (12500, 32), jnp.float32)
        src = jax.random.randint(jax.random.fold_in(_gk, 2), (400000,), 0, 12500, jnp.int32)
        dst = jax.random.randint(jax.random.fold_in(_gk, 3), (400000,), 0, 12500, jnp.int32)
        _o = jnp.argsort(dst, stable=True)
        src = src[_o]
        dst = dst[_o]
        edge_attr_32 = -9.77346e-05 + 0.999888 * jax.random.normal(jax.random.fold_in(_gk, 12), (400000, 32), jnp.float32)
        node_vec1 = jax.random.uniform(jax.random.fold_in(_gk, 13), (12500, 1), jnp.float32, 0.0, 0.999991)
        node_vec1_n2 = jax.random.uniform(jax.random.fold_in(_gk, 14), (12500, 1), jnp.float32, 0.0, 0.999991)
        return (x, src, dst, edge_attr_32, node_vec1, node_vec1_n2)
    x, src, dst, edge_attr_32, node_vec1, node_vec1_n2 = _rec_inputs()

    def _L0_gnn_setup():
        import jax, jax.numpy as jnp
        import numpy as np
        N_NODES = 12500
        N_EDGES = 200000
        D_FEAT = 32
        key = jax.random.key(seed)
        k1, k2, k3, k4, k5 = jax.random.split(key, 5)
        src_feats = jax.random.normal(k1, (N_NODES, D_FEAT), dtype=jnp.float32)
        cj = jax.random.uniform(k2, (N_NODES, 1), dtype=jnp.float32)
        ci = jax.random.uniform(k3, (N_NODES, 1), dtype=jnp.float32)
        src_idx = jax.random.randint(k4, (N_EDGES,), 0, N_NODES, dtype=jnp.int32)
        dst_idx = jax.random.randint(k5, (N_EDGES,), 0, N_NODES, dtype=jnp.int32)
        return {'src_feats': src_feats, 'cj': cj, 'ci': ci, 'src_idx': src_idx, 'dst_idx': dst_idx}
    _L0_gnn_all = _L0_gnn_setup()
    _L0_gnn_in = {k: v for k, v in _L0_gnn_all.items() if k in ()}
    del _L0_gnn_all

    def _L1_gnn_setup():
        import jax, jax.numpy as jnp
        import numpy as np
        N_NODES = 6250
        N_EDGES = 200000
        D_FEAT = 32
        key = jax.random.key(seed)
        k1, k2, k3, k4 = jax.random.split(key, 4)
        node_feat = jax.random.normal(k1, (N_NODES, D_FEAT), dtype=jnp.float32)
        edge_feat = jax.random.normal(k2, (N_EDGES, D_FEAT), dtype=jnp.float32)
        eps = jnp.zeros((1,), dtype=jnp.float32)
        src = jax.random.randint(k3, (N_EDGES,), 0, N_NODES, dtype=jnp.int64)
        dst = jax.random.randint(k4, (N_EDGES,), 0, N_NODES, dtype=jnp.int64)
        return {'node_feat': node_feat, 'edge_feat': edge_feat, 'eps': eps, 'src': src, 'dst': dst}
    _L1_gnn_all = _L1_gnn_setup()
    _L1_gnn_in = {k: v for k, v in _L1_gnn_all.items() if k in ('eps',)}
    del _L1_gnn_all
    return {'x': x, 'src': src, 'dst': dst, 'edge_attr_32': edge_attr_32, 'node_vec1': node_vec1, 'node_vec1_n2': node_vec1_n2, 'L1_gnn_eps': _L1_gnn_in['eps']}

def reference(x, src, dst, edge_attr_32, node_vec1, node_vec1_n2, L1_gnn_eps):
    import jax
    import jax.numpy as jnp

    def _L0_gnn_ref(src_feats, cj, ci, src_idx, dst_idx):
        import jax, jax.numpy as jnp
        import numpy as np
        N_NODES = 12500
        N_EDGES = 200000
        D_FEAT = 32
        weighted = src_feats * cj
        msgs = weighted[src_idx]
        agg = jax.ops.segment_sum(msgs, dst_idx, num_segments=N_NODES)
        return agg * ci

    def _L1_gnn_ref(node_feat, edge_feat, eps, src, dst):
        import jax, jax.numpy as jnp
        import numpy as np
        N_NODES = 6250
        N_EDGES = 200000
        D_FEAT = 32
        m = jax.nn.relu(node_feat[src] + edge_feat)
        neigh = jax.ops.segment_sum(m, dst, num_segments=node_feat.shape[0])
        return (1.0 + eps[0]) * node_feat + neigh
    h = jnp.maximum(_layernorm(x, axis=-1), 0.0)
    x = x + _L0_gnn_ref(h, node_vec1, node_vec1_n2, src, dst)
    h = jnp.maximum(_layernorm(x, axis=-1), 0.0)
    x = x + _L1_gnn_ref(h, edge_attr_32, L1_gnn_eps, src, dst)
    return x

_drawn_inputs = setup_inputs


def setup_inputs(seed=0):
    import zlib

    import numpy as np

    out = dict(_drawn_inputs(seed))
    spreads = {}
    factors = {}
    for name, (base, spread) in spreads.items():
        noise = np.random.default_rng([zlib.crc32(name.encode()), seed]).standard_normal(out[name].shape)
        drawn = base * np.exp(spread * noise) if base else spread * noise
        out[name] = jnp.asarray(drawn.astype(out[name].dtype))
    for name, factor in factors.items():
        out[name] = (out[name] * factor).astype(out[name].dtype)
    return out
```

```python
import concourse.bass as bass
from concourse import mybir
from contextlib import ExitStack

F32 = mybir.dt.float32
I32 = mybir.dt.int32
ALU = mybir.AluOpType
ACT = mybir.ActivationFunctionType
AX = mybir.AxisListType.X

LN_EPS = 1e-5


def gnn_two_layers(nc, x, src, dst, edge_attr, node_vec1, node_vec1_n2, eps, out):
    N, F = x.shape
    E = src.shape[0]
    P = 128
    TILES = 25
    SUPER = P * TILES
    NS = E // SUPER
    assert E == NS * SUPER and NS % 2 == 1 and NS <= P
    SLOTS = 2
    WINDOW = 128
    NP = 125
    C = N // NP
    CHUNKS = 4
    CC = C // CHUNKS
    assert N == NP * C and C == CHUNKS * CC
    WINDOWS = -(-N // WINDOW)
    ACC = N + WINDOW
    LAYERS = 2
    GATHERED = 16 * TILES
    LOADS = [2, 3]

    def done(s):
        return s + SLOTS + 1

    def freed(s):
        return s + 1

    src_v = src.rearrange("(r j) -> r j", j=TILES)
    dst_v = dst.rearrange("(r j) -> r j", j=TILES)
    attr_v = edge_attr.rearrange("(r j) f -> r (j f)", j=TILES)
    dst_rows_v = dst.rearrange("(s e) -> s e", e=SUPER)
    x_v = x.rearrange("(p c) f -> p c f", c=C)
    out_v = out.rearrange("(p c) f -> p c f", c=C)
    cj_v = node_vec1.rearrange("(p c) o -> p (c o)", c=C)
    ci_v = node_vec1_n2.rearrange("(p c) o -> p (c o)", c=C)

    tables = [nc.dram_tensor(f"table{l}", (N, F), F32, kind="Internal").ap() for l in range(LAYERS)]
    tables_v = [t.rearrange("(p c) f -> p c f", c=C) for t in tables]

    ctx = ExitStack()
    with ctx:
        def sb(name, shape, dt=F32):
            return ctx.enter_context(nc.sbuf_tensor(name, shape, dt))

        def pb(name, shape):
            return ctx.enter_context(nc.psum_tensor(name, shape, F32))

        def sem(name):
            return ctx.enter_context(nc.semaphore(name))

        ident = sb("ident", [P, P])
        iota_sb = sb("iota_sb", [P, WINDOW])
        window_start = sb("window_start", [P, WINDOWS])
        ln_eps = sb("ln_eps", [P, 1])
        eps_in = sb("eps_in", [NP, 1])
        eps1 = sb("eps1", [NP, 1])
        xs = sb("xs", [NP, C, F])
        centered = sb("centered", [NP, C, F])
        squares = sb("squares", [NP, CC, F])
        table_sb = sb("table_sb", [NP, C, F])
        result = sb("result", [NP, C, F])
        sums = sb("sums", [NP, C])
        mean = sb("mean", [NP, C])
        sumsq = sb("sumsq", [NP, C])
        std = sb("std", [NP, C])
        rstd = sb("rstd", [NP, C])
        cj = sb("cj", [NP, C])
        ci = sb("ci", [NP, C])
        dst_rows = sb("dst_rows", [NS, SUPER], I32)
        lowest = sb("lowest", [NS, 1])
        highest = sb("highest", [NS, 1])
        span = sb("span", [NS, 1])
        beyond = sb("beyond", [NS, 1])
        spread = sb("spread", [NS, 2, P])
        base = sb("base", [P, NS])
        base_i = sb("base_i", [P, NS], I32)
        any_beyond = sb("any_beyond", [P, 1])
        any_beyond_i = sb("any_beyond_i", [P, 1], I32)
        src_i = sb("src_i", [P, SLOTS, TILES], I32)
        dst_i = sb("dst_i", [P, SLOTS, TILES], I32)
        key = sb("key", [P, SLOTS, TILES])
        far = sb("far", [P, TILES])
        far_dst = sb("far_dst", [P, TILES])
        rows = sb("rows", [P, SLOTS, TILES, F])
        attr = sb("attr", [P, SLOTS, TILES * F])
        onehot = sb("onehot", [P, SLOTS, TILES, WINDOW])
        acc = sb("acc", [F, ACC])

        BANK = 512
        iota = pb("iota", [P, BANK])[:, 0:WINDOW]
        agg = [pb(f"agg{k}", [P, BANK])[0:F, 0:WINDOW] for k in range(SLOTS)]
        nodes_ps = [pb(f"nodes_ps{k}", [P, 2 * BANK]) for k in range(2)]
        spread_ps = [nodes_ps[k][:, 0:NS] for k in range(2)]

        def nodes_in(k):
            return nodes_ps[k % 2][0:NP, 0:CC * F].rearrange("p (c f) -> p c f", f=F)

        x_loaded = [sem(f"x_loaded{k}") for k in range(CHUNKS)]
        small_loaded = sem("small_loaded")
        dst_rows_loaded = sem("dst_rows_loaded")
        pool_steps = sem("pool_steps")
        gathers_begun = sem("gathers_begun")
        consts_ready = sem("consts_ready")
        ln_eps_ready = sem("ln_eps_ready")
        dve_steps = sem("dve_steps")
        var_ready = sem("var_ready")
        std_ready = sem("std_ready")
        table_ready = sem("table_ready")
        table_stored = [sem(f"table_stored{l}") for l in range(LAYERS)]
        spread_ready = sem("spread_ready")
        base_spread = sem("base_spread")
        flag_ready = sem("flag_ready")
        loaded = [[sem(f"loaded{l}_{k}") for k in range(SLOTS)] for l in range(LAYERS)]
        gathered = [[sem(f"gathered{l}_{k}") for k in range(SLOTS)] for l in range(LAYERS)]
        key_ready = [sem(f"key_ready{l}") for l in range(LAYERS)]
        onehot_ready = [sem(f"onehot_ready{l}") for l in range(LAYERS)]
        rows_added = sem("rows_added")
        messages_ready = sem("messages_ready")
        agg_ready = [sem(f"agg_ready{l}") for l in range(LAYERS)]
        acc_added = [sem(f"acc_added{l}") for l in range(LAYERS)]
        acc_final = sem("acc_final")
        nodes_ready = sem("nodes_ready")
        nodes_used = sem("nodes_used")
        result_ready = sem("result_ready")
        out_stored = sem("out_stored")
        far_loaded = [sem(f"far_loaded{l}") for l in range(LAYERS)]
        far_gathered = [sem(f"far_gathered{l}") for l in range(LAYERS)]
        far_steps = [sem(f"far_steps{l}") for l in range(LAYERS)]
        far_rows_added = sem("far_rows_added")
        far_messages = sem("far_messages")
        far_key = [sem(f"far_key{l}") for l in range(LAYERS)]
        far_onehot = [sem(f"far_onehot{l}") for l in range(LAYERS)]
        far_agg = [sem(f"far_agg{l}") for l in range(LAYERS)]
        far_added = [sem(f"far_added{l}") for l in range(LAYERS)]

        block = ctx.enter_context(nc.Block())

        def chunk(k):
            return slice(k * CC, (k + 1) * CC)

        def per_node(t, k):
            return t[:, chunk(k)].unsqueeze(2).to_broadcast([NP, CC, F])

        def edge_rows(s):
            return bass.ds(s * P, P)

        def over_supertiles(eng, step):
            with eng.Fori(0, NS // SLOTS) as i:
                for slot in range(SLOTS):
                    step(i * SLOTS + slot, slot, i)
            step(NS - 1, 0, NS // SLOTS)

        def spread_beyond(eng):
            eng.wait_ge(flag_ready, 1)
            return eng.value_load(any_beyond_i[0:1, 0:1], min_val=0, max_val=1)

        @block.sync
        def _(sp):
            for k in range(CHUNKS):
                sp.dma_start(xs[:, chunk(k), :], x_v[:, chunk(k), :]).then_inc(x_loaded[k], 16)
            sp.dma_start(cj[:], cj_v).then_inc(small_loaded, 16)
            sp.dma_start(ci[:], ci_v).then_inc(small_loaded, 16)
            sp.dma_start(eps_in[:], eps.partition_broadcast(NP)).then_inc(small_loaded, 16)
            sp.dma_start(dst_rows[:], dst_rows_v).then_inc(dst_rows_loaded, 16)

            def load(l, s, slot, landed):
                sp.dma_start(src_i[:, slot, :], src_v[edge_rows(s), :]).then_inc(landed, 16)
                sp.dma_start(dst_i[:, slot, :], dst_v[edge_rows(s), :]).then_inc(landed, 16)
                if l == 1:
                    sp.dma_start(attr[:, slot, :], attr_v[edge_rows(s), :]).then_inc(landed, 16)

            for l in range(LAYERS):
                def step(s, slot, use):
                    sp.wait_ge(agg_ready[l], freed(s))
                    load(l, s, slot, loaded[l][slot])
                over_supertiles(sp, step)
                sp.wait_ge(agg_ready[l], done(NS - 1))
                with sp.If(spread_beyond(sp) > 0):
                    with sp.Fori(0, NS) as s:
                        sp.wait_ge(far_added[l], s * WINDOWS + 1)
                        load(l, s, 0, far_loaded[l])
                    sp.wait_ge(far_added[l], NS * WINDOWS + 1)

        @block.gpsimd
        def _(pool):
            pool.memset(ln_eps[:], LN_EPS).then_inc(ln_eps_ready, 1)
            pool.memset(ident[:], 0.0).then_inc(pool_steps, 1)
            pool.iota(iota_sb[:], pattern=[[1, WINDOW]], base=0, channel_multiplier=0,
                      allow_small_or_imprecise_dtypes=True).then_inc(consts_ready, 1)
            pool.iota(window_start[:], pattern=[[WINDOW, WINDOWS]], base=0, channel_multiplier=0,
                      allow_small_or_imprecise_dtypes=True).then_inc(consts_ready, 1)
            pool.wait_ge(pool_steps, 1)
            pool.affine_select(out=ident[:], in_=ident[:], compare_op=ALU.not_equal, fill=1.0, base=0,
                               pattern=[[-1, P]], channel_multiplier=1).then_inc(consts_ready, 1)

            def gather(l, slot, landed):
                pool.sem_inc(gathers_begun, 1)
                for j in range(TILES):
                    pool.indirect_dma_start(
                        rows[:, slot, j, :], None, tables[l],
                        bass.IndirectOffsetOnAxis(ap=src_i[:, slot, j:j + 1], axis=0),
                    ).then_inc(landed, 16)

            for l in range(LAYERS):
                def step(s, slot, use):
                    pool.wait_ge(loaded[l][slot], 16 * LOADS[l] * (use + 1))
                    pool.wait_ge(agg_ready[0] if l == 0 else rows_added, freed(s))
                    pool.wait_ge(table_stored[l], 16 * CHUNKS)
                    gather(l, slot, gathered[l][slot])
                over_supertiles(pool, step)
                with pool.If(spread_beyond(pool) > 0):
                    with pool.Fori(0, NS) as s:
                        pool.wait_ge(far_loaded[l], 16 * LOADS[l] * (s + 1))
                        pool.wait_ge(table_stored[l], 16 * CHUNKS)
                        gather(l, 0, far_gathered[l])

        @block.scalar
        def _(act):
            act.wait_ge(ln_eps_ready, 1)

            def deviation(l, k):
                act.wait_ge(var_ready, l * CHUNKS + k + 1)
                nc.scalar.activation(std[:, chunk(k)], sumsq[:, chunk(k)], ACT.Sqrt, bias=ln_eps[0:NP, 0:1],
                                     scale=1.0 / F).then_inc(std_ready, 1)

            for l in range(LAYERS):
                deviation(l, 0)
                for k in range(CHUNKS):
                    if k + 1 < CHUNKS:
                        deviation(l, k + 1)
                    act.wait_ge(table_ready, l * CHUNKS + k + 1)
                    act.dma_start(tables_v[l][:, chunk(k), :], table_sb[:, chunk(k), :]).then_inc(table_stored[l], 16)
                act.wait_ge(table_stored[l], 16 * CHUNKS)

            act.sem_inc(messages_ready, SLOTS)

            def step(s, slot, use):
                act.wait_ge(rows_added, done(s))
                nc.scalar.activation(attr[:, slot, :], attr[:, slot, :], ACT.Relu).then_inc(messages_ready, 1)
            over_supertiles(act, step)
            with act.If(spread_beyond(act) > 0):
                with act.Fori(0, NS) as s:
                    act.wait_ge(far_rows_added, s + 1)
                    nc.scalar.activation(attr[:, 0, :], attr[:, 0, :], ACT.Relu).then_inc(far_messages, 1)

            for k in range(CHUNKS):
                act.wait_ge(result_ready, k + 1)
                act.dma_start(out_v[:, chunk(k), :], result[:, chunk(k), :]).then_inc(out_stored, 16)
            act.wait_ge(out_stored, 16 * CHUNKS)

        @block.tensor
        def _(pe):
            for l in range(LAYERS):
                pe.sem_inc(agg_ready[l], SLOTS)
            pe.wait_ge(spread_ready, 2)
            pe.wait_ge(consts_ready, 3)
            for k in range(2):
                nc.tensor.matmul(spread_ps[k], spread[:, k, :], ident[0:NS, 0:NS], start=True,
                                 stop=True).then_inc(base_spread, 1)

            def products(l, slot, out_ps, finished):
                for j in range(TILES):
                    message = rows[:, slot, j, :] if l == 0 else attr[:, slot, j * F:(j + 1) * F]
                    last = nc.tensor.matmul(out_ps, message, onehot[:, slot, j, :], start=(j == 0),
                                            stop=(j == TILES - 1))
                last.then_inc(finished, 1)

            for l in range(LAYERS):
                def step(s, slot, use):
                    pe.wait_ge(onehot_ready[l], done(s))
                    if l == 0:
                        pe.wait_ge(gathered[l][slot], GATHERED * (use + 1))
                    else:
                        pe.wait_ge(messages_ready, done(s))
                    pe.wait_ge(acc_added[l], freed(s))
                    products(l, slot, agg[slot], agg_ready[l])
                over_supertiles(pe, step)
                with pe.If(spread_beyond(pe) > 0):
                    with pe.Fori(0, NS) as s:
                        with pe.Fori(0, WINDOWS) as w:
                            if l == 0:
                                pe.wait_ge(far_gathered[l], GATHERED * (s + 1))
                            else:
                                pe.wait_ge(far_messages, s + 1)
                            pe.wait_ge(far_onehot[l], s * WINDOWS + w + 1)
                            pe.wait_ge(far_added[l], s * WINDOWS + w + 1)
                            products(l, 0, agg[0], far_agg[l])
                pe.wait_ge(acc_final, l + 1)
                for k in range(CHUNKS):
                    pe.wait_ge(nodes_used, max(1, l * CHUNKS + k))
                    for c in range(CC):
                        node = k * CC + c
                        last = nc.tensor.transpose(nodes_in(k)[:, c, :], acc[:, node:node + C * (NP - 1) + 1:C],
                                                   ident[0:F, 0:F])
                    last.then_inc(nodes_ready, 1)

        @block.vector
        def _(dve):
            steps = [0]

            def link(ins):
                steps[0] += 1
                ins.then_inc(dve_steps, 1)
                dve.wait_ge(dve_steps, steps[0])

            def center(l, k):
                link(nc.vector.reduce_sum(sums[:, chunk(k)], xs[:, chunk(k), :], AX))
                link(nc.vector.tensor_scalar(mean[:, chunk(k)], sums[:, chunk(k)], 1.0 / F, None, ALU.mult))
                link(nc.vector.tensor_tensor(centered[:, chunk(k), :], xs[:, chunk(k), :], per_node(mean, k), ALU.subtract))
                link(nc.vector.tensor_tensor(squares[:], centered[:, chunk(k), :], centered[:, chunk(k), :], ALU.mult))
                nc.vector.reduce_sum(sumsq[:, chunk(k)], squares[:], AX).then_inc(var_ready, 1)
                dve.wait_ge(var_ready, l * CHUNKS + k + 1)

            def table_rows(l, k):
                dve.wait_ge(std_ready, l * CHUNKS + k + 1)
                link(nc.vector.reciprocal(rstd[:, chunk(k)], std[:, chunk(k)]))
                if l == 0:
                    link(nc.vector.tensor_tensor(rstd[:, chunk(k)], rstd[:, chunk(k)], cj[:, chunk(k)], ALU.mult))
                nc.vector.scalar_tensor_tensor(table_sb[:, chunk(k), :], centered[:, chunk(k), :], 0.0,
                                               per_node(rstd, k), ALU.max, ALU.mult).then_inc(table_ready, 1)

            dve.wait_ge(x_loaded[0], 16)
            center(0, 0)
            for k in range(CHUNKS):
                if k == 0:
                    dve.wait_ge(small_loaded, 48)
                if k + 1 < CHUNKS:
                    dve.wait_ge(x_loaded[k + 1], 16)
                    center(0, k + 1)
                table_rows(0, k)
            link(nc.vector.tensor_scalar(eps1[:], eps_in[:], 1.0, None, ALU.add))

            dve.wait_ge(consts_ready, 3)
            link(nc.vector.tensor_copy(iota, iota_sb[:]))
            dve.wait_ge(dst_rows_loaded, 16)
            link(nc.vector.tensor_reduce(lowest[:], dst_rows[:], AX, ALU.min))
            link(nc.vector.tensor_reduce(highest[:], dst_rows[:], AX, ALU.max))
            link(nc.vector.tensor_tensor(span[:], highest[:], lowest[:], ALU.subtract))
            link(nc.vector.tensor_scalar(beyond[:], span[:], float(WINDOW), None, ALU.is_ge))
            nc.vector.tensor_copy(spread[:, 0, :], lowest[:].to_broadcast([NS, P])).then_inc(spread_ready, 1)
            nc.vector.tensor_copy(spread[:, 1, :], beyond[:].to_broadcast([NS, P])).then_inc(spread_ready, 1)
            dve.wait_ge(base_spread, 2)
            link(nc.vector.tensor_copy(base[:], spread_ps[0]))
            nc.vector.tensor_copy(base_i[:], spread_ps[0]).then_inc(nodes_used, 1)
            link(nc.vector.reduce_max(any_beyond[:], spread_ps[1], AX))
            nc.vector.tensor_copy(any_beyond_i[:], any_beyond[:]).then_inc(flag_ready, 1)
            dve.wait_ge(nodes_used, 1)

            for l in range(LAYERS):
                dve.sem_inc(key_ready[l], SLOTS)
                dve.sem_inc(onehot_ready[l], SLOTS)
                if l == 1:
                    dve.sem_inc(rows_added, SLOTS)
                nc.vector.memset(acc[:], 0.0).then_inc(acc_added[l], SLOTS)

                def one_hot(slot, ready):
                    nc.vector.tensor_tensor(
                        onehot[:, slot, :, :], iota.unsqueeze(1).to_broadcast([P, TILES, WINDOW]),
                        key[:, slot, :].unsqueeze(2).to_broadcast([P, TILES, WINDOW]), ALU.is_equal).then_inc(ready, 1)

                def add_rows(slot, added):
                    nc.vector.tensor_tensor(attr[:, slot, :], attr[:, slot, :],
                                            rows[:, slot, :, :].rearrange("p j f -> p (j f)"), ALU.add).then_inc(added, 1)

                def step(s, slot, use):
                    dve.wait_ge(loaded[l][slot], 16 * LOADS[l] * (use + 1))
                    nc.vector.tensor_scalar(key[:, slot, :], dst_i[:, slot, :], base[:, bass.ds(s, 1)], None,
                                            ALU.subtract).then_inc(key_ready[l], 1)
                    dve.wait_ge(key_ready[l], done(s))
                    one_hot(slot, onehot_ready[l])
                    if l == 1:
                        dve.wait_ge(gathered[l][slot], GATHERED * (use + 1))
                        add_rows(slot, rows_added)
                    first = dve.value_load(base_i[0:1, bass.ds(s, 1)], min_val=0, max_val=N - 1)
                    dve.wait_ge(agg_ready[l], done(s))
                    dve.wait_ge(acc_added[l], s + SLOTS)
                    window = acc[:, bass.ds(first, WINDOW)]
                    nc.vector.tensor_tensor(window, window, agg[slot], ALU.add).then_inc(acc_added[l], 1)
                over_supertiles(dve, step)
                dve.wait_ge(acc_added[l], NS + SLOTS)

                with dve.If(spread_beyond(dve) > 0):
                    dve.sem_inc(far_added[l], 1)
                    with dve.Fori(0, NS) as s:
                        dve.wait_ge(far_loaded[l], 16 * LOADS[l] * (s + 1))
                        nc.vector.tensor_scalar(far[:], dst_i[:, 0, :], base[:, bass.ds(s, 1)], float(WINDOW),
                                                ALU.subtract, ALU.is_ge).then_inc(far_steps[l], 1)
                        dve.wait_ge(far_steps[l], 2 * s + 1)
                        nc.vector.scalar_tensor_tensor(far_dst[:], dst_i[:, 0, :], 1.0, far[:], ALU.add,
                                                       ALU.mult).then_inc(far_steps[l], 1)
                        if l == 1:
                            dve.wait_ge(far_gathered[l], GATHERED * (s + 1))
                            add_rows(0, far_rows_added)
                        with dve.Fori(0, WINDOWS) as w:
                            nth = s * WINDOWS + w + 1
                            dve.wait_ge(far_steps[l], 2 * s + 2)
                            nc.vector.tensor_scalar(key[:, 0, :], far_dst[:], window_start[:, bass.ds(w, 1)], 1.0,
                                                    ALU.subtract, ALU.subtract).then_inc(far_key[l], 1)
                            dve.wait_ge(far_key[l], nth)
                            one_hot(0, far_onehot[l])
                            dve.wait_ge(far_agg[l], nth)
                            dve.wait_ge(far_added[l], nth)
                            window = acc[:, bass.ds(w * WINDOW, WINDOW)]
                            nc.vector.tensor_tensor(window, window, agg[0], ALU.add).then_inc(far_added[l], 1)
                    dve.wait_ge(far_added[l], NS * WINDOWS + 1)
                dve.sem_inc(acc_final, 1)

                def read_nodes(k):
                    dve.wait_ge(nodes_ready, l * CHUNKS + k + 1)

                if l == 0:
                    def x1(k):
                        read_nodes(k)
                        nc.vector.tensor_tensor(squares[:], nodes_in(k), per_node(ci, k), ALU.mult).then_inc(nodes_used, 1)
                        dve.wait_ge(nodes_used, k + 2)
                        link(nc.vector.tensor_tensor(xs[:, chunk(k), :], xs[:, chunk(k), :], squares[:], ALU.add))
                        center(1, k)
                    dve.wait_ge(table_stored[0], 16 * CHUNKS)
                    x1(0)
                    for k in range(CHUNKS):
                        if k + 1 < CHUNKS:
                            x1(k + 1)
                        table_rows(1, k)
                    dve.wait_ge(table_ready, 2 * CHUNKS)
                    link(nc.vector.scalar_tensor_tensor(
                        result[:], table_sb[:], eps1[:, 0:1], xs[:], ALU.mult, ALU.add))
                else:
                    for k in range(CHUNKS):
                        read_nodes(k)
                        nc.vector.tensor_tensor(result[:, chunk(k), :], result[:, chunk(k), :], nodes_in(k),
                                                ALU.add).then_inc(nodes_used, 1)
                        dve.wait_ge(nodes_used, CHUNKS + k + 2)
                        dve.sem_inc(result_ready, 1)


_INS = ['x', 'src', 'dst', 'edge_attr_32', 'node_vec1', 'node_vec1_n2', 'L1_gnn_eps']


def kernel(**inputs):
    import numpy as np
    import concourse.bacc as bacc
    from concourse.bass_utils import run_bass_kernel_spmd

    nc = bacc.Bacc("TRN2", target_bir_lowering=False, num_devices=1)
    arrays, args = {}, []
    for name in _INS:
        a = np.ascontiguousarray(inputs[name])
        arrays[f"in_{name}"] = a
        args.append(nc.dram_tensor(f"in_{name}", a.shape, mybir.dt.from_np(a.dtype), kind="ExternalInput").ap())
    out = nc.dram_tensor("out", inputs['x'].shape, F32, kind="ExternalOutput").ap()
    gnn_two_layers(nc, *args, out)
    r = run_bass_kernel_spmd(nc, [arrays], core_ids=[0])
    return r.results[0]["out"]
```

```python
import concourse.bass as bass
from concourse import mybir
from contextlib import ExitStack

F32 = mybir.dt.float32
I32 = mybir.dt.int32
F16 = mybir.dt.float16
BF16 = mybir.dt.bfloat16
ALU = mybir.AluOpType
ACT = mybir.ActivationFunctionType
AX = mybir.AxisListType.X

LN_EPS = 1e-5


def gnn_two_layers(nc, x, src, dst, edge_attr, node_vec1, node_vec1_n2, eps, out):
    N, F = x.shape
    E = src.shape[0]
    P = 128
    TILES = 25
    PT = 4
    GT = TILES - PT
    SUPER = P * TILES
    NS = E // SUPER
    SLOTS = 2
    assert E == NS * SUPER and NS % SLOTS == 1 and 3 < NS <= P
    WINDOW = 128
    NP = 125
    C = N // NP
    CHUNKS = 4
    CC = C // CHUNKS
    assert N == NP * C and C == CHUNKS * CC
    WINDOWS = -(-N // WINDOW)
    ACC = N + WINDOW
    LAYERS = 2
    S = 3
    J = 5
    G = C // J
    GC = CC // J
    assert C == G * J and CC == GC * J
    WIDE = F * S * J
    BATCH = 4
    BATCHES = G // BATCH
    assert G == BATCHES * BATCH
    MIDDLE = G // 2
    ROUND = 1.5 * 2.0 ** 23
    GATHERED = 16 * GT
    LOADS = [1, 2]

    def done(s):
        return s + SLOTS + 1

    def freed(s):
        return s + 1

    src_v = src.rearrange("(r j) -> r j", j=TILES)
    attr_v = edge_attr.rearrange("(r j) f -> r (j f)", j=TILES)
    src_pv = src.rearrange("(s p j) -> p s j", p=P, j=TILES)
    dst_pv = dst.rearrange("(s p j) -> p s j", p=P, j=TILES)
    x_v = x.rearrange("(p c) f -> p c f", c=C)
    out_v = out.rearrange("(p c) f -> p c f", c=C)
    cj_v = node_vec1.rearrange("(p c) o -> p (c o)", c=C)
    ci_v = node_vec1_n2.rearrange("(p c) o -> p (c o)", c=C)

    tables = [nc.dram_tensor(f"table{l}", (N, F), F32, kind="Internal").ap() for l in range(LAYERS)]
    tables_v = [t.rearrange("(p c) f -> p c f", c=C) for t in tables]

    ctx = ExitStack()
    with ctx:
        def sb(name, shape, dt=F32):
            return ctx.enter_context(nc.sbuf_tensor(name, shape, dt))

        def pb(name, shape, dt=F32):
            return ctx.enter_context(nc.psum_tensor(name, shape, dt))

        def sem(name):
            return ctx.enter_context(nc.semaphore(name))

        ident = sb("ident", [P, P])
        ident16 = sb("ident16", [P, P], F16)
        join = sb("join", [F * S, F])
        iota_sb = sb("iota_sb", [P, WINDOW])
        window_start = sb("window_start", [P, WINDOWS])
        group_key = sb("group_key", [NP, G])
        ln_eps = sb("ln_eps", [P, 1])
        eps_in = sb("eps_in", [NP, 1])
        eps1 = sb("eps1", [NP, 1])
        xs = sb("xs", [NP, C, F])
        centered = sb("centered", [NP, C, F])
        squares = sb("squares", [NP, CC, F])
        sums = sb("sums", [NP, C])
        mean = sb("mean", [NP, C])
        sumsq = sb("sumsq", [NP, C])
        std = sb("std", [NP, C])
        rstd = sb("rstd", [NP, C])
        cj = sb("cj", [NP, C])
        ci = sb("ci", [NP, C])
        parts = sb("parts", [NP, G * WIDE], BF16)
        parts_v = parts[:].rearrange("p (g f s j) -> p g j f s", f=F, s=S, j=J)
        src_pe = sb("src_pe", [P, NS, PT], I32)
        src_key = sb("src_key", [P, NS * PT], F16)
        member = sb("member", [P, NS * PT, J], BF16)
        key = sb("key", [P, NS, TILES])
        dst_all = key[:].bitcast(I32)
        ends = sb("ends", [P, 2, NS])
        ends_of = sb("ends_of", [NS, 2])
        span = sb("span", [NS, 1])
        beyond = sb("beyond", [NS, 1])
        spread = sb("spread", [NS, 2, P])
        base = sb("base", [P, NS])
        base1 = sb("base1", [P, NS])
        base_i = sb("base_i", [P, NS], I32)
        any_beyond = sb("any_beyond", [P, 1])
        any_beyond_i = sb("any_beyond_i", [P, 1], I32)
        src_i = sb("src_i", [P, SLOTS, TILES], I32)
        rows = sb("rows", [P, SLOTS, TILES, F])
        attr = sb("attr", [P, SLOTS, TILES, F])
        message = sb("message", [P, SLOTS, TILES * F, S], BF16)
        src_onehot = sb("src_onehot", [NP, SLOTS, G, PT * P], BF16)
        picked = sb("picked", [P, PT, F, S * J])
        dst_onehot = sb("dst_onehot", [P, SLOTS, TILES, WINDOW], BF16)
        room = dst_onehot[:].rearrange("p a b c -> p (a b c)").bitcast(F32)
        row_of, col_of, group_of, scaled = (room[:, k * NS * PT:(k + 1) * NS * PT] for k in range(4))
        acc = sb("acc", [F * S, ACC])
        far = sb("far", [P, TILES])
        far_dst = sb("far_dst", [P, TILES])
        far_key = sb("far_key", [P, TILES])

        BANK = 512
        candidates = pb("candidates", [P, PT, BANK])
        agg_ps = pb("agg_ps", [P, BANK])
        agg = [agg_ps[0:F * S, k * WINDOW:(k + 1) * WINDOW] for k in range(SLOTS)]
        iota = pb("iota", [P, BANK])[:, 0:WINDOW]
        key_rows = [pb(f"key_rows{k}", [P, 2 * BANK], F16)[0:NP, 0:PT * P] for k in range(SLOTS)]
        low_ps, high_ps = candidates[0:NS, 0, 0:P], candidates[0:NS, 1, 0:P]
        spread_ps = [candidates[:, 2 + k, 0:NS] for k in range(2)]

        def nodes_in(k):
            pair = candidates[0:NP, 2 * (k % 2):2 * (k % 2) + 2, :].rearrange("p b n -> p (b n)")
            return pair[:, 0:CC * F].rearrange("p (c f) -> p c f", f=F)

        def per_layer(name):
            return [sem(f"{name}{l}") for l in range(LAYERS)]

        def per_slot(name):
            return [[sem(f"{name}{l}_{k}") for k in range(SLOTS)] for l in range(LAYERS)]

        x_loaded = [sem(f"x_loaded{k}") for k in range(CHUNKS)]
        small_loaded = sem("small_loaded")
        src_pe_loaded = sem("src_pe_loaded")
        dst_loaded = sem("dst_loaded")
        pool_steps = sem("pool_steps")
        gathers_begun = sem("gathers_begun")
        consts_ready = sem("consts_ready")
        ln_eps_ready = sem("ln_eps_ready")
        dve_steps = sem("dve_steps")
        var_ready = sem("var_ready")
        std_ready = sem("std_ready")
        table_ready = sem("table_ready")
        table_stored = per_layer("table_stored")
        parts_ready = sem("parts_ready")
        src_key_ready = sem("src_key_ready")
        ends_ready = sem("ends_ready")
        ends_turned = sem("ends_turned")
        spread_ready = sem("spread_ready")
        base_spread = sem("base_spread")
        flag_ready = sem("flag_ready")
        loaded = per_slot("loaded")
        gathered = per_slot("gathered")
        key_rows_ready = per_layer("key_rows_ready")
        src_onehot_ready = per_layer("src_onehot_ready")
        candidates_ready = per_layer("candidates_ready")
        picked_ready = per_layer("picked_ready")
        rows_ready = per_layer("rows_ready")
        rows_added = sem("rows_added")
        message1_ready = per_layer("message1_ready")
        message1_left = per_layer("message1_left")
        message2_ready = per_layer("message2_ready")
        messages_ready = per_layer("messages_ready")
        agg_ready = per_layer("agg_ready")
        acc_zeroed = sem("acc_zeroed")
        acc_added = per_layer("acc_added")
        acc_final = sem("acc_final")
        nodes_ready = sem("nodes_ready")
        nodes_used = sem("nodes_used")
        result_ready = sem("result_ready")
        out_stored = sem("out_stored")
        far_loaded = per_layer("far_loaded")
        far_gathered = per_layer("far_gathered")
        far_steps = per_layer("far_steps")
        far_added_rows = sem("far_added_rows")
        far_message1 = per_layer("far_message1")
        far_left = per_layer("far_left")
        far_message2 = per_layer("far_message2")
        far_messages = per_layer("far_messages")
        far_key_ready = per_layer("far_key_ready")
        far_onehot = per_layer("far_onehot")
        far_agg = per_layer("far_agg")
        far_added = per_layer("far_added")

        block = ctx.enter_context(nc.Block())

        def chunk(k):
            return slice(k * CC, (k + 1) * CC)

        def per_node(t, k):
            return t[:, chunk(k)].unsqueeze(2).to_broadcast([NP, CC, F])

        def edge_rows(s):
            return bass.ds(s * P, P)

        def over_supertiles(eng, step):
            step(0, 0, 0, 2)
            with eng.Fori(0, (NS - 3) // 2) as i:
                step(2 * i + 1, 1, i, 2)
                step(2 * i + 2, 0, i + 1, 2)
            step(NS - 2, 1, (NS - 3) // 2, 1)
            step(NS - 1, 0, (NS - 1) // 2, 0)

        def spread_beyond(eng):
            eng.wait_ge(flag_ready, 1)
            return eng.value_load(any_beyond_i[0:1, 0:1], min_val=0, max_val=1)

        def summed(l, slot):
            return (rows if l == 0 else attr)[:, slot, :, :].rearrange("p j f -> p (j f)")

        @block.sync
        def _(sp):
            for k in range(CHUNKS):
                sp.dma_start(xs[:, chunk(k), :], x_v[:, chunk(k), :]).then_inc(x_loaded[k], 16)
            sp.dma_start(cj[:], cj_v).then_inc(small_loaded, 16)
            sp.dma_start(ci[:], ci_v).then_inc(small_loaded, 16)
            sp.dma_start(eps_in[:], eps.partition_broadcast(NP)).then_inc(small_loaded, 16)
            sp.dma_start(src_pe[:], src_pv[:, :, GT:TILES]).then_inc(src_pe_loaded, 16)

            def load(l, s, slot, landed):
                sp.dma_start(src_i[:, slot, :], src_v[edge_rows(s), :]).then_inc(landed, 16)
                if l == 1:
                    sp.dma_start(attr[:, slot, :, :].rearrange("p j f -> p (j f)"),
                                 attr_v[edge_rows(s), :]).then_inc(landed, 16)

            for l in range(LAYERS):
                def step(s, slot, use, left):
                    sp.wait_ge(messages_ready[l], freed(s))
                    load(l, s, slot, loaded[l][slot])
                    if l == 0 and isinstance(s, int) and s == 0:
                        sp.dma_start(dst_all, dst_pv).then_inc(dst_loaded, 16)
                over_supertiles(sp, step)
                sp.wait_ge(messages_ready[l], done(NS - 1))
                with sp.If(spread_beyond(sp) > 0):
                    with sp.Fori(0, NS) as s:
                        sp.wait_ge(far_added[l], s * WINDOWS + 1)
                        load(l, s, 0, far_loaded[l])
                    sp.wait_ge(far_added[l], NS * WINDOWS + 1)

        @block.gpsimd
        def _(pool):
            pool.memset(ln_eps[:], LN_EPS).then_inc(ln_eps_ready, 1)
            pool.memset(ident[:], 0.0).then_inc(pool_steps, 1)
            pool.memset(join[:], 1.0).then_inc(pool_steps, 1)
            pool.iota(iota_sb[:], pattern=[[1, WINDOW]], base=0, channel_multiplier=0,
                      allow_small_or_imprecise_dtypes=True).then_inc(consts_ready, 1)
            pool.iota(window_start[:], pattern=[[WINDOW, WINDOWS]], base=0, channel_multiplier=0,
                      allow_small_or_imprecise_dtypes=True).then_inc(consts_ready, 1)
            pool.iota(group_key[:], pattern=[[P, G]], base=-MIDDLE * P, channel_multiplier=1,
                      allow_small_or_imprecise_dtypes=True).then_inc(consts_ready, 1)
            pool.wait_ge(pool_steps, 2)
            pool.affine_select(out=ident[:], in_=ident[:], compare_op=ALU.not_equal, fill=1.0, base=0,
                               pattern=[[-1, P]], channel_multiplier=1).then_inc(consts_ready, 1)
            pool.affine_select(out=join[:], in_=join[:], compare_op=ALU.is_ge, fill=0.0, base=0,
                               pattern=[[-S, F]], channel_multiplier=1).then_inc(pool_steps, 1)
            pool.wait_ge(pool_steps, 3)
            pool.affine_select(out=join[:], in_=join[:], compare_op=ALU.is_ge, fill=0.0, base=S - 1,
                               pattern=[[S, F]], channel_multiplier=-1).then_inc(consts_ready, 1)

            def gather(l, slot, tiles, landed):
                pool.sem_inc(gathers_begun, 1)
                for j in range(tiles):
                    pool.indirect_dma_start(
                        rows[:, slot, j, :], None, tables[l],
                        bass.IndirectOffsetOnAxis(ap=src_i[:, slot, j:j + 1], axis=0),
                    ).then_inc(landed, 16)

            for l in range(LAYERS):
                if l == 1:
                    pool.wait_ge(nodes_ready, CHUNKS)
                pool.memset(acc[:], 0.0).then_inc(acc_zeroed, 1)

                def step(s, slot, use, left):
                    pool.wait_ge(loaded[l][slot], 16 * LOADS[l] * (use + 1))
                    pool.wait_ge(messages_ready[l], freed(s))
                    pool.wait_ge(table_stored[l], 16 * CHUNKS)
                    gather(l, slot, GT, gathered[l][slot])
                over_supertiles(pool, step)
                with pool.If(spread_beyond(pool) > 0):
                    with pool.Fori(0, NS) as s:
                        pool.wait_ge(far_loaded[l], 16 * LOADS[l] * (s + 1))
                        gather(l, 0, TILES, far_gathered[l])

        @block.scalar
        def _(act):
            act.wait_ge(ln_eps_ready, 1)

            def deviation(l, k):
                act.wait_ge(var_ready, l * CHUNKS + k + 1)
                nc.scalar.activation(std[:, chunk(k)], sumsq[:, chunk(k)], ACT.Sqrt, bias=ln_eps[0:NP, 0:1],
                                     scale=1.0 / F).then_inc(std_ready, 1)

            def first_part(l, slot, ready):
                nc.scalar.activation(message[:, slot, :, 0], summed(l, slot),
                                     ACT.Copy if l == 0 else ACT.Relu).then_inc(ready, 1)

            def second_part(l, slot, ready):
                nc.scalar.activation(message[:, slot, :, 1], summed(l, slot), ACT.Copy).then_inc(ready, 1)

            for l in range(LAYERS):
                deviation(l, 0)
                for k in range(CHUNKS):
                    if k + 1 < CHUNKS:
                        deviation(l, k + 1)
                    act.wait_ge(table_ready, l * CHUNKS + k + 1)
                    act.dma_start(tables_v[l][:, chunk(k), :], centered[:, chunk(k), :]).then_inc(table_stored[l], 16)
                def step(s, slot, use, left):
                    if l == 0:
                        act.wait_ge(gathered[l][slot], GATHERED * (use + 1))
                        act.wait_ge(rows_ready[l], s + 1)
                    else:
                        act.wait_ge(rows_added, s + 1)
                    first_part(l, slot, message1_ready[l])
                    act.wait_ge(message1_left[l], s + 1)
                    second_part(l, slot, message2_ready[l])
                over_supertiles(act, step)
                with act.If(spread_beyond(act) > 0):
                    with act.Fori(0, NS) as s:
                        if l == 0:
                            act.wait_ge(far_gathered[l], 16 * TILES * (s + 1))
                        else:
                            act.wait_ge(far_added_rows, s + 1)
                        first_part(l, 0, far_message1[l])
                        act.wait_ge(far_left[l], s + 1)
                        second_part(l, 0, far_message2[l])

            for k in range(CHUNKS):
                act.wait_ge(result_ready, k + 1)
                act.dma_start(out_v[:, chunk(k), :], xs[:, chunk(k), :]).then_inc(out_stored, 16)
            act.wait_ge(out_stored, 16 * CHUNKS)

        @block.tensor
        def _(pe):
            pe.wait_ge(consts_ready, 5)
            pe.wait_ge(ends_ready, 2)
            for k, turned in enumerate((low_ps, high_ps)):
                nc.tensor.transpose(turned, ends[:, k, :], ident[:]).then_inc(ends_turned, 1)
            pe.wait_ge(spread_ready, 2)
            for k in range(2):
                nc.tensor.matmul(spread_ps[k], spread[:, k, :], ident[0:NS, 0:NS], start=True,
                                 stop=True).then_inc(base_spread, 1)

            def products(slot, out_ps, finished):
                for j in range(TILES):
                    last = nc.tensor.matmul(out_ps, message[:, slot, j * F:(j + 1) * F, :].rearrange("p f s -> p (f s)"),
                                            dst_onehot[:, slot, j, :], start=(j == 0), stop=(j == TILES - 1))
                last.then_inc(finished, 1)

            for l in range(LAYERS):
                def keys(s, slot):
                    for t in range(PT):
                        column = src_key[:, bass.ds(s * PT + t, 1)].to_broadcast([P, NP])
                        last = nc.tensor.transpose(key_rows[slot][:, t * P:(t + 1) * P], column, ident16[:])
                    last.then_inc(key_rows_ready[l], 1)

                def candidate_rows(s, slot):
                    for g in range(G):
                        if g % BATCH == 0:
                            pe.wait_ge(src_onehot_ready[l], s * BATCHES + g // BATCH + 1)
                        for t in range(PT):
                            last = nc.tensor.matmul(candidates[:, t, 0:WIDE], src_onehot[:, slot, g, t * P:(t + 1) * P],
                                                    parts[:, g * WIDE:(g + 1) * WIDE], start=(g == 0), stop=(g == G - 1))
                    last.then_inc(candidates_ready[l], 1)

                pe.wait_ge(src_key_ready, 2)
                pe.wait_ge(nodes_used, 1 if l == 0 else 1 + CHUNKS)
                keys(0, 0)
                keys(1, 1)
                pe.wait_ge(parts_ready, (l + 1) * CHUNKS)
                candidate_rows(0, 0)

                def step(s, slot, use, left):
                    if left == 2:
                        keys(s + 2, slot)
                    if left >= 1:
                        pe.wait_ge(picked_ready[l], s + 1)
                        candidate_rows(s + 1, 1 - slot)
                    pe.wait_ge(messages_ready[l], done(s))
                    products(slot, agg[slot], agg_ready[l])
                over_supertiles(pe, step)
                with pe.If(spread_beyond(pe) > 0):
                    with pe.Fori(0, NS) as s:
                        with pe.Fori(0, WINDOWS) as w:
                            pe.wait_ge(far_messages[l], s + 1)
                            pe.wait_ge(far_onehot[l], s * WINDOWS + w + 1)
                            pe.wait_ge(far_added[l], s * WINDOWS + w + 1)
                            products(0, agg[0], far_agg[l])
                pe.wait_ge(acc_final, l + 1)
                for k in range(CHUNKS):
                    pe.wait_ge(nodes_used, max(1, l * CHUNKS + k))
                    for c in range(CC):
                        node = k * CC + c
                        last = nc.tensor.matmul(nodes_in(k)[:, c, :], acc[:, node:node + C * (NP - 1) + 1:C],
                                                join[:], start=True, stop=True)
                    last.then_inc(nodes_ready, 1)

        @block.vector
        def _(dve):
            steps = [0]

            def link(ins):
                steps[0] += 1
                ins.then_inc(dve_steps, 1)
                dve.wait_ge(dve_steps, steps[0])

            def center(l, k):
                link(nc.vector.reduce_sum(sums[:, chunk(k)], xs[:, chunk(k), :], AX))
                link(nc.vector.tensor_scalar(mean[:, chunk(k)], sums[:, chunk(k)], 1.0 / F, None, ALU.mult))
                link(nc.vector.tensor_tensor(centered[:, chunk(k), :], xs[:, chunk(k), :], per_node(mean, k), ALU.subtract))
                link(nc.vector.tensor_tensor(squares[:], centered[:, chunk(k), :], centered[:, chunk(k), :], ALU.mult))
                nc.vector.reduce_sum(sumsq[:, chunk(k)], squares[:], AX).then_inc(var_ready, 1)
                dve.wait_ge(var_ready, l * CHUNKS + k + 1)

            def table_rows(l, k):
                dve.wait_ge(std_ready, l * CHUNKS + k + 1)
                link(nc.vector.reciprocal(rstd[:, chunk(k)], std[:, chunk(k)]))
                if l == 0:
                    link(nc.vector.tensor_tensor(rstd[:, chunk(k)], rstd[:, chunk(k)], cj[:, chunk(k)], ALU.mult))
                nc.vector.scalar_tensor_tensor(centered[:, chunk(k), :], centered[:, chunk(k), :], 0.0,
                                               per_node(rstd, k), ALU.max, ALU.mult).then_inc(table_ready, 1)

            def table_parts(l):
                dve.wait_ge(table_ready, (l + 1) * CHUNKS)
                for k in range(CHUNKS):
                    part = [parts_v[:, k * GC:(k + 1) * GC, :, :, i] for i in range(S)]
                    whole = centered[:, chunk(k), :].rearrange("p (g j) f -> p g j f", j=J)
                    left = squares[:].rearrange("p (g j) f -> p g j f", j=J)
                    link(nc.vector.tensor_copy(part[0], whole))
                    link(nc.vector.tensor_tensor(left, whole, part[0], ALU.subtract))
                    link(nc.vector.tensor_copy(part[1], left))
                    nc.vector.tensor_tensor(part[2], left, part[1], ALU.subtract).then_inc(parts_ready, 1)
                    dve.wait_ge(parts_ready, l * CHUNKS + k + 1)

            for l in range(LAYERS):
                dve.sem_inc(messages_ready[l], SLOTS)

            dve.wait_ge(x_loaded[0], 16)
            center(0, 0)
            for k in range(CHUNKS):
                if k == 0:
                    dve.wait_ge(small_loaded, 48)
                if k + 1 < CHUNKS:
                    dve.wait_ge(x_loaded[k + 1], 16)
                    center(0, k + 1)
                table_rows(0, k)
            link(nc.vector.tensor_scalar(eps1[:], eps_in[:], 1.0, None, ALU.add))

            dve.wait_ge(consts_ready, 5)
            nc.vector.tensor_copy(ident16[:], ident[:]).then_inc(src_key_ready, 1)
            link(nc.vector.tensor_copy(iota, iota_sb[:]))
            dve.wait_ge(src_pe_loaded, 16)
            src_flat = src_pe[:].rearrange("p s t -> p (s t)")
            link(nc.vector.tensor_scalar(scaled, src_flat, 1.0 / C, 0.5 / C - 0.5, ALU.mult, ALU.add))
            link(nc.vector.tensor_scalar(row_of, scaled, ROUND, ROUND, ALU.add, ALU.subtract))
            link(nc.vector.scalar_tensor_tensor(col_of, row_of, -float(C), src_flat, ALU.mult, ALU.add))
            link(nc.vector.tensor_scalar(scaled, col_of, 1.0 / J, 0.5 / J - 0.5, ALU.mult, ALU.add))
            link(nc.vector.tensor_scalar(group_of, scaled, ROUND, ROUND, ALU.add, ALU.subtract))
            link(nc.vector.scalar_tensor_tensor(col_of, group_of, -float(J), col_of, ALU.mult, ALU.add))
            link(nc.vector.tensor_scalar(group_of, group_of, float(P), -float(MIDDLE * P), ALU.mult, ALU.add))
            nc.vector.tensor_tensor(src_key[:], group_of, row_of, ALU.add).then_inc(src_key_ready, 1)
            link(nc.vector.tensor_tensor(
                member[:], iota_sb[:, 0:J].unsqueeze(1).to_broadcast([P, NS * PT, J]),
                col_of.unsqueeze(2).to_broadcast([P, NS * PT, J]), ALU.is_equal))
            table_parts(0)

            dve.wait_ge(dst_loaded, 16)
            nc.vector.tensor_reduce(ends[:, 0, :], dst_all, AX, ALU.min).then_inc(ends_ready, 1)
            nc.vector.tensor_reduce(ends[:, 1, :], dst_all, AX, ALU.max).then_inc(ends_ready, 1)
            dve.wait_ge(ends_turned, 2)
            link(nc.vector.tensor_reduce(ends_of[:, 0:1], low_ps, AX, ALU.min))
            link(nc.vector.tensor_reduce(ends_of[:, 1:2], high_ps, AX, ALU.max))
            link(nc.vector.tensor_tensor(span[:], ends_of[:, 1:2], ends_of[:, 0:1], ALU.subtract))
            link(nc.vector.tensor_scalar(beyond[:], span[:], float(WINDOW), None, ALU.is_ge))
            nc.vector.tensor_copy(spread[:, 0, :], ends_of[:, 0:1].to_broadcast([NS, P])).then_inc(spread_ready, 1)
            nc.vector.tensor_copy(spread[:, 1, :], beyond[:].to_broadcast([NS, P])).then_inc(spread_ready, 1)
            dve.wait_ge(base_spread, 2)
            link(nc.vector.tensor_copy(base[:], spread_ps[0]))
            link(nc.vector.tensor_copy(base_i[:], spread_ps[0]))
            link(nc.vector.reduce_max(any_beyond[:], spread_ps[1], AX))
            nc.vector.tensor_copy(any_beyond_i[:], any_beyond[:]).then_inc(flag_ready, 1)
            dve.sem_inc(nodes_used, 1)
            link(nc.vector.tensor_scalar(base1[:], base[:], 1.0, None, ALU.add))
            link(nc.vector.tensor_tensor(key[:], dst_all, base[:].unsqueeze(2).to_broadcast([P, NS, TILES]), ALU.subtract))

            for l in range(LAYERS):
                def src_onehots(s, slot):
                    dve.wait_ge(key_rows_ready[l], s + 1)
                    for g in range(G):
                        one = nc.vector.tensor_scalar(src_onehot[:, slot, g, :], key_rows[slot], group_key[:, g:g + 1],
                                                      None, ALU.is_equal)
                        if g % BATCH == BATCH - 1:
                            one.then_inc(src_onehot_ready[l], 1)

                def dst_onehots(slot, keys):
                    return nc.vector.tensor_tensor(
                        dst_onehot[:, slot, :, :], iota.unsqueeze(1).to_broadcast([P, TILES, WINDOW]),
                        keys.unsqueeze(2).to_broadcast([P, TILES, WINDOW]), ALU.is_equal)

                def add_rows(slot, added):
                    nc.vector.tensor_tensor(attr[:, slot, :, :], attr[:, slot, :, :], rows[:, slot, :, :],
                                            ALU.add).then_inc(added, 1)

                def after_first_part(slot, ready):
                    if l == 0:
                        nc.vector.tensor_tensor(summed(l, slot), summed(l, slot), message[:, slot, :, 0],
                                                ALU.subtract).then_inc(ready, 1)
                    else:
                        nc.vector.scalar_tensor_tensor(summed(l, slot), summed(l, slot), 0.0, message[:, slot, :, 0],
                                                       ALU.max, ALU.subtract).then_inc(ready, 1)

                def third_part(slot, ready):
                    nc.vector.tensor_tensor(message[:, slot, :, 2], summed(l, slot), message[:, slot, :, 1],
                                            ALU.subtract).then_inc(ready, 1)

                def add_window(s, slot):
                    first = dve.value_load(base_i[0:1, bass.ds(s, 1)], min_val=0, max_val=N - 1)
                    dve.wait_ge(agg_ready[l], s + 1)
                    dve.wait_ge(acc_added[l], s + 1)
                    window = acc[:, bass.ds(first, WINDOW)]
                    nc.vector.tensor_tensor(window, window, agg[slot], ALU.add).then_inc(acc_added[l], 1)

                src_onehots(0, 0)
                dve.wait_ge(acc_zeroed, l + 1)
                dve.sem_inc(acc_added[l], 1)

                def step(s, slot, use, left):
                    if left >= 1:
                        src_onehots(s + 1, 1 - slot)
                    dve.wait_ge(candidates_ready[l], s + 1)
                    nc.vector.tensor_tensor(
                        picked[:].rearrange("p t f k -> p t (f k)").rearrange("p t (q j) -> p t q j", j=J),
                        candidates[:, :, 0:WIDE].rearrange("p t (q j) -> p t q j", j=J),
                        member[:, bass.ds(s * PT, PT), :].unsqueeze(2).to_broadcast([P, PT, F * S, J]),
                        ALU.mult).then_inc(picked_ready[l], 1)
                    dve.wait_ge(picked_ready[l], s + 1)
                    nc.vector.reduce_sum(rows[:, slot, GT:TILES, :], picked[:], AX).then_inc(rows_ready[l], 1)
                    if l == 1:
                        dve.wait_ge(rows_ready[l], s + 1)
                        dve.wait_ge(gathered[l][slot], GATHERED * (use + 1))
                        dve.wait_ge(loaded[l][slot], 16 * LOADS[l] * (use + 1))
                        add_rows(slot, rows_added)
                    dst_onehots(slot, key[:, bass.ds(s, 1), :].rearrange("p o j -> p (o j)"))
                    dve.wait_ge(message1_ready[l], s + 1)
                    after_first_part(slot, message1_left[l])
                    if not (isinstance(s, int) and s == 0):
                        add_window(s - 1, 1 - slot)
                    dve.wait_ge(message2_ready[l], s + 1)
                    third_part(slot, messages_ready[l])
                over_supertiles(dve, step)
                add_window(NS - 1, 0)
                dve.wait_ge(acc_added[l], NS + 1)

                with dve.If(spread_beyond(dve) > 0):
                    dve.sem_inc(far_added[l], 1)
                    with dve.Fori(0, NS) as s:
                        if l == 0:
                            dve.wait_ge(far_gathered[l], 16 * TILES * (s + 1))
                        else:
                            dve.wait_ge(far_gathered[l], 16 * TILES * (s + 1))
                            add_rows(0, far_added_rows)
                        keys = key[:, bass.ds(s, 1), :].rearrange("p o j -> p (o j)")
                        nc.vector.tensor_scalar(far[:], keys, float(WINDOW), None, ALU.is_ge).then_inc(far_steps[l], 1)
                        dve.wait_ge(far_steps[l], 2 * s + 1)
                        nc.vector.scalar_tensor_tensor(far_dst[:], keys, base1[:, bass.ds(s, 1)], far[:], ALU.add,
                                                       ALU.mult).then_inc(far_steps[l], 1)
                        dve.wait_ge(far_message1[l], s + 1)
                        after_first_part(0, far_left[l])
                        dve.wait_ge(far_message2[l], s + 1)
                        third_part(0, far_messages[l])
                        with dve.Fori(0, WINDOWS) as w:
                            nth = s * WINDOWS + w + 1
                            dve.wait_ge(far_steps[l], 2 * s + 2)
                            nc.vector.tensor_scalar(far_key[:], far_dst[:], window_start[:, bass.ds(w, 1)], 1.0,
                                                    ALU.subtract, ALU.subtract).then_inc(far_key_ready[l], 1)
                            dve.wait_ge(far_key_ready[l], nth)
                            dst_onehots(0, far_key[:]).then_inc(far_onehot[l], 1)
                            dve.wait_ge(far_agg[l], nth)
                            dve.wait_ge(far_added[l], nth)
                            window = acc[:, bass.ds(w * WINDOW, WINDOW)]
                            nc.vector.tensor_tensor(window, window, agg[0], ALU.add).then_inc(far_added[l], 1)
                    dve.wait_ge(far_added[l], NS * WINDOWS + 1)
                dve.sem_inc(acc_final, 1)

                def read_nodes(k):
                    dve.wait_ge(nodes_ready, l * CHUNKS + k + 1)

                if l == 0:
                    def x1(k):
                        read_nodes(k)
                        nc.vector.tensor_tensor(squares[:], nodes_in(k), per_node(ci, k), ALU.mult).then_inc(nodes_used, 1)
                        dve.wait_ge(nodes_used, k + 2)
                        link(nc.vector.tensor_tensor(xs[:, chunk(k), :], xs[:, chunk(k), :], squares[:], ALU.add))
                        center(1, k)
                    dve.wait_ge(table_stored[0], 16 * CHUNKS)
                    x1(0)
                    for k in range(CHUNKS):
                        if k + 1 < CHUNKS:
                            x1(k + 1)
                        table_rows(1, k)
                    table_parts(1)
                    link(nc.vector.scalar_tensor_tensor(xs[:], centered[:], eps1[:, 0:1], xs[:], ALU.mult, ALU.add))
                else:
                    for k in range(CHUNKS):
                        read_nodes(k)
                        nc.vector.tensor_tensor(xs[:, chunk(k), :], xs[:, chunk(k), :], nodes_in(k),
                                                ALU.add).then_inc(nodes_used, 1)
                        dve.wait_ge(nodes_used, CHUNKS + k + 2)
                        dve.sem_inc(result_ready, 1)


_INS = ['x', 'src', 'dst', 'edge_attr_32', 'node_vec1', 'node_vec1_n2', 'L1_gnn_eps']


def kernel(**inputs):
    import numpy as np
    import concourse.bacc as bacc
    from concourse.bass_utils import run_bass_kernel_spmd

    nc = bacc.Bacc("TRN2", target_bir_lowering=False, num_devices=1)
    arrays, args = {}, []
    for name in _INS:
        a = np.ascontiguousarray(inputs[name])
        arrays[f"in_{name}"] = a
        args.append(nc.dram_tensor(f"in_{name}", a.shape, mybir.dt.from_np(a.dtype), kind="ExternalInput").ap())
    out = nc.dram_tensor("out", inputs['x'].shape, F32, kind="ExternalOutput").ap()
    gnn_two_layers(nc, *args, out)
    r = run_bass_kernel_spmd(nc, [arrays], core_ids=[0])
    return r.results[0]["out"]
```

```python
import concourse.bass as bass
from concourse import mybir
from contextlib import ExitStack

F32 = mybir.dt.float32
I32 = mybir.dt.int32
F16 = mybir.dt.float16
BF16 = mybir.dt.bfloat16
ALU = mybir.AluOpType
ACT = mybir.ActivationFunctionType
AX = mybir.AxisListType.X

LN_EPS = 1e-5


def gnn_two_layers(nc, x, src, dst, edge_attr, node_vec1, node_vec1_n2, eps, out):
    N, F = x.shape
    E = src.shape[0]
    P = 128
    TILES = 25
    PT = [5, 5, 4, 5, 5, 4]
    ROUND = len(PT)
    PTMAX = max(PT)
    EARLY = 3
    GT = [TILES - n for n in PT]
    SUPER = P * TILES
    NS = E // SUPER
    ROUNDS = (NS - 4) // ROUND
    SLOTS = 2
    assert E == NS * SUPER and ROUND % SLOTS == 0 and ROUND + 4 <= NS <= P and (NS - 1) % SLOTS == 0
    WINDOW = 128
    NP = 125
    C = N // NP
    CHUNKS = 4
    CC = C // CHUNKS
    assert N == NP * C and C == CHUNKS * CC
    WINDOWS = -(-N // WINDOW)
    ACC = N + WINDOW
    LAYERS = 2
    S = 3
    J = 5
    G = C // J
    GC = CC // J
    assert C == G * J and CC == GC * J
    WIDE = F * S * J
    BATCH = 4
    ACT_BATCHES = 2
    DVE_BATCHES = G // BATCH - ACT_BATCHES
    DVE_GROUPS = DVE_BATCHES * BATCH
    assert G % BATCH == 0
    MIDDLE = G // 2
    TO_INTEGER = 1.5 * 2.0 ** 23
    LOADS = [1, 2]

    def done(s):
        return s + SLOTS + 1

    def whole(s):
        return isinstance(s, int) and s in (0, NS - 1)

    def uses(phase, r):
        return r * (ROUND // SLOTS) + phase // SLOTS

    def gathers(s, phase, r):
        slot = phase % SLOTS
        more = (TILES - GT[0] if slot == 0 else 0) + (TILES - GT[phase] if whole(s) and s > 0 else 0)
        return 16 * (r * sum(GT[slot::SLOTS]) + sum(GT[slot:phase + 1:SLOTS]) + more)

    def freed(s):
        return s + 1

    src_v = src.rearrange("(r j) -> r j", j=TILES)
    attr_v = edge_attr.rearrange("(r j) f -> r (j f)", j=TILES)
    src_pv = src.rearrange("(s p j) -> p s j", p=P, j=TILES)
    dst_pv = dst.rearrange("(s p j) -> p s j", p=P, j=TILES)
    x_v = x.rearrange("(p c) f -> p c f", c=C)
    out_v = out.rearrange("(p c) f -> p c f", c=C)
    cj_v = node_vec1.rearrange("(p c) o -> p (c o)", c=C)
    ci_v = node_vec1_n2.rearrange("(p c) o -> p (c o)", c=C)

    tables = [nc.dram_tensor(f"table{l}", (N, F), F32, kind="Internal").ap() for l in range(LAYERS)]
    tables_v = [t.rearrange("(p c) f -> p c f", c=C) for t in tables]

    ctx = ExitStack()
    with ctx:
        def sb(name, shape, dt=F32):
            return ctx.enter_context(nc.sbuf_tensor(name, shape, dt))

        def pb(name, shape, dt=F32):
            return ctx.enter_context(nc.psum_tensor(name, shape, dt))

        def sem(name):
            return ctx.enter_context(nc.semaphore(name))

        ident = sb("ident", [P, P])
        ident16 = sb("ident16", [P, P], F16)
        join = sb("join", [F * S, F])
        iota_sb = sb("iota_sb", [P, WINDOW])
        window_start = sb("window_start", [P, WINDOWS])
        group_key = sb("group_key", [NP, G])
        less_group_key = sb("less_group_key", [NP, G])
        one = sb("one", [P, 1])
        ln_eps = sb("ln_eps", [P, 1])
        root_eps = sb("root_eps", [P, 1])
        zero = sb("zero", [P, 1])
        eps_in = sb("eps_in", [NP, 1])
        eps1 = sb("eps1", [NP, 1])
        xs = sb("xs", [NP, C, F])
        centered = sb("centered", [NP, C, F])
        sums = sb("sums", [NP, C])
        mean = sb("mean", [NP, C])
        sumsq = sb("sumsq", [NP, C])
        std = sb("std", [NP, C])
        rstd = sb("rstd", [NP, C])
        cj = sb("cj", [NP, C])
        ci = sb("ci", [NP, C])
        parts = sb("parts", [NP, G * WIDE], BF16)
        parts_v = parts[:].rearrange("p (g f s j) -> p g j f s", f=F, s=S, j=J)
        src_key = sb("src_key", [P, NS * PTMAX], F16)
        member_of = sb("member_of", [P, NS * PTMAX], F16)
        member = sb("member", [P, PTMAX, J], BF16)
        key = sb("key", [P, NS, TILES])
        dst_all = key[:].bitcast(I32)
        base = sb("base", [P, NS])
        base1 = sb("base1", [P, NS])
        base_i = sb("base_i", [P, NS], I32)
        any_beyond = sb("any_beyond", [P, 1])
        any_beyond_i = sb("any_beyond_i", [P, 1], I32)
        src_i = sb("src_i", [P, SLOTS, TILES], I32)
        rows = sb("rows", [P, SLOTS, TILES, F])
        attr = sb("attr", [P, SLOTS, TILES, F])
        message_room = sb("message", [P, SLOTS * TILES * F * S], BF16)
        message = message_room[:].rearrange("p (a e s) -> p a e s", a=SLOTS, s=S)
        src_onehot = [sb(f"src_onehot{k}", [NP, G, PTMAX * P], BF16) for k in range(SLOTS)]
        pieces = src_onehot[0][:].rearrange("p g e -> p (g e)").bitcast(F32).rearrange("p (k c f) -> p k c f", c=CC, f=F)
        product = [pieces[:, k, :, :] for k in range(CHUNKS)]
        squares = [pieces[:, CHUNKS + k, :, :] for k in range(CHUNKS)]
        pieces = message_room[0:NP, :].bitcast(F32).rearrange("p (k n) -> p k n", n=CC * F)
        left_over = [pieces[:, k, :].rearrange("p (g j f) -> p g j f", j=J, f=F) for k in range(3)]
        key_copy = sb("key_copy", [NP, PTMAX * P], F16)
        picked = sb("picked", [P, PTMAX * WIDE], BF16)
        dst_onehot = sb("dst_onehot", [P, SLOTS, TILES, WINDOW], BF16)
        room = dst_onehot[:].rearrange("p a b c -> p (a b c)").bitcast(F32)
        EDGES = NS * PTMAX
        row_of, col_of, group_of, scaled = (room[:, k * EDGES:(k + 1) * EDGES] for k in range(4))
        room = attr[:].rearrange("p a b c -> p (a b c)")
        src_pe = room[:, 0:EDGES].bitcast(I32).rearrange("p (s t) -> p s t", t=PTMAX)
        room = room[:, EDGES:]
        ends = room[:, 0:2 * NS].rearrange("p (k s) -> p k s", k=2)
        spread = room[0:NS, 2 * NS:2 * NS + 2 * P].rearrange("p (k c) -> p k c", k=2)
        ends_of, span, beyond = (room[0:NS, 2 * NS + 2 * P + k:2 * NS + 2 * P + k + n] for k, n in ((0, 2), (2, 1), (3, 1)))
        window_sums = sb("window_sums", [F * S, WINDOW])
        acc = sb("acc", [F, ACC])
        room = picked[:].bitcast(F32)
        far, far_dst, far_key = (room[:, k * TILES:(k + 1) * TILES] for k in range(3))

        BANK = 512
        candidates = pb("candidates", [P, PTMAX, BANK])
        agg_ps = pb("agg_ps", [P, BANK])
        agg = agg_ps[0:F * S, 0:WINDOW]
        joined = agg_ps[0:F, WINDOW:2 * WINDOW]
        key_banks = [pb(f"key_rows{k}", [P, 2 * BANK], F16) for k in range(SLOTS)]
        key_rows = [key_banks[k][0:NP, 0:PTMAX * P] for k in range(SLOTS)]
        iota = key_banks[1][:, 2 * (BANK - WINDOW):].bitcast(F32)
        low_ps, high_ps = (agg_ps[0:NS, k * P:(k + 1) * P] for k in range(2))
        spread_ps = [agg_ps[:, 2 * P + k * NS:2 * P + (k + 1) * NS] for k in range(2)]

        def nodes_in(k):
            pair = candidates[0:NP, 2 * (k % 2):2 * (k % 2) + 2, :].rearrange("p b n -> p (b n)")
            return pair[:, 0:CC * F].rearrange("p (c f) -> p c f", f=F)

        def per_layer(name):
            return [sem(f"{name}{l}") for l in range(LAYERS)]

        def per_slot(name):
            return [[sem(f"{name}{l}_{k}") for k in range(SLOTS)] for l in range(LAYERS)]

        x_loaded = [sem(f"x_loaded{k}") for k in range(CHUNKS)]
        small_loaded = sem("small_loaded")
        src_pe_loaded = sem("src_pe_loaded")
        dst_loaded = sem("dst_loaded")
        pool_steps = sem("pool_steps")
        gathers_begun = sem("gathers_begun")
        consts_ready = sem("consts_ready")
        ln_eps_ready = sem("ln_eps_ready")
        dve_steps = sem("dve_steps")
        product_ready = sem("product_ready")
        x1_ready = sem("x1_ready")
        mean_ready = sem("mean_ready")
        centered_ready = sem("centered_ready")
        last_centered = sem("last_centered")
        squares_ready = sem("squares_ready")
        var_ready = sem("var_ready")
        std_ready = sem("std_ready")
        table_ready = sem("table_ready")
        table_stored = per_layer("table_stored")
        part1_ready = sem("part1_ready")
        parts_ready = sem("parts_ready")
        src_key_ready = sem("src_key_ready")
        ends_ready = sem("ends_ready")
        ends_turned = sem("ends_turned")
        spread_ready = sem("spread_ready")
        base_spread = sem("base_spread")
        flag_ready = sem("flag_ready")
        loaded = per_slot("loaded")
        gathered = per_slot("gathered")
        key_rows_ready = per_layer("key_rows_ready")
        src_onehot_ready = per_layer("src_onehot_ready")
        act_onehot_ready = per_layer("act_onehot_ready")
        key_copied = per_layer("key_copied")
        distance_ready = per_layer("distance_ready")
        early_candidates = per_layer("early_candidates")
        late_candidates = per_layer("late_candidates")
        member_ready = per_layer("member_ready")
        early_picked = per_layer("early_picked")
        late_picked = per_layer("late_picked")
        rows_ready = per_layer("rows_ready")
        rows_added = sem("rows_added")
        message1_ready = per_layer("message1_ready")
        message1_left = per_layer("message1_left")
        message2_ready = per_layer("message2_ready")
        messages_ready = per_layer("messages_ready")
        agg_ready = per_layer("agg_ready")
        agg_copied = per_layer("agg_copied")
        joined_ready = per_layer("joined_ready")
        acc_zeroed = sem("acc_zeroed")
        acc_added = per_layer("acc_added")
        acc_final = sem("acc_final")
        nodes_ready = sem("nodes_ready")
        nodes_used = sem("nodes_used")
        result_ready = sem("result_ready")
        out_stored = sem("out_stored")
        far_loaded = per_layer("far_loaded")
        far_gathered = per_layer("far_gathered")
        far_steps = per_layer("far_steps")
        far_added_rows = sem("far_added_rows")
        far_message1 = per_layer("far_message1")
        far_left = per_layer("far_left")
        far_message2 = per_layer("far_message2")
        far_messages = per_layer("far_messages")
        far_key_ready = per_layer("far_key_ready")
        far_onehot = per_layer("far_onehot")
        far_agg = per_layer("far_agg")
        far_copied = per_layer("far_copied")
        far_joined = per_layer("far_joined")
        far_added = per_layer("far_added")

        block = ctx.enter_context(nc.Block())

        def chunk(k):
            return slice(k * CC, (k + 1) * CC)

        HELPED = CHUNKS - 1

        def center(eng, k):
            return eng.tensor_tensor(centered[:, chunk(k), :], xs[:, chunk(k), :], per_node(mean, k), ALU.subtract)

        def add_product(eng, k):
            return eng.tensor_tensor(xs[:, chunk(k), :], xs[:, chunk(k), :], product[k], ALU.add)

        def per_node(t, k):
            return t[:, chunk(k)].unsqueeze(2).to_broadcast([NP, CC, F])

        def edge_rows(s):
            return bass.ds(s * P, P)

        def over_supertiles(eng, step):
            step(0, 0, 0, 4)
            with eng.Fori(0, ROUNDS) as r:
                for phase in range(1, ROUND):
                    step(r * ROUND + phase, phase, r, 4)
                step((r + 1) * ROUND, 0, r + 1, 4)
            for s in range(ROUNDS * ROUND + 1, NS):
                step(s, s % ROUND, s // ROUND, min(NS - 1 - s, 4))

        def spread_beyond(eng):
            eng.wait_ge(flag_ready, 1)
            return eng.value_load(any_beyond_i[0:1, 0:1], min_val=0, max_val=1)

        def summed(l, slot):
            return (rows if l == 0 else attr)[:, slot, :, :].rearrange("p j f -> p (j f)")

        @block.sync
        def _(sp):
            for k in range(CHUNKS):
                sp.dma_start(xs[:, chunk(k), :], x_v[:, chunk(k), :]).then_inc(x_loaded[k], 16)
            sp.dma_start(cj[:], cj_v).then_inc(small_loaded, 16)
            sp.dma_start(ci[:], ci_v).then_inc(small_loaded, 16)
            sp.dma_start(eps_in[:], eps.partition_broadcast(NP)).then_inc(small_loaded, 16)
            sp.dma_start(src_pe, src_pv[:, :, TILES - PTMAX:TILES]).then_inc(src_pe_loaded, 16)

            def load(l, s, slot, landed):
                sp.dma_start(src_i[:, slot, :], src_v[edge_rows(s), :]).then_inc(landed, 16)
                if l == 1:
                    sp.dma_start(attr[:, slot, :, :].rearrange("p j f -> p (j f)"),
                                 attr_v[edge_rows(s), :]).then_inc(landed, 16)

            for l in range(LAYERS):
                def step(s, phase, r, left):
                    slot = phase % SLOTS
                    sp.wait_ge(messages_ready[l], freed(s))
                    load(l, s, slot, loaded[l][slot])
                over_supertiles(sp, step)
                sp.wait_ge(messages_ready[l], done(NS - 1))
                with sp.If(spread_beyond(sp) > 0):
                    with sp.Fori(0, NS) as s:
                        sp.wait_ge(far_added[l], s * WINDOWS + 1)
                        load(l, s, 0, far_loaded[l])
                    sp.wait_ge(far_added[l], NS * WINDOWS + 1)

        @block.gpsimd
        def _(pool):
            pool.memset(zero[:], 0.0).then_inc(ln_eps_ready, 1)
            pool.memset(ln_eps[:], LN_EPS).then_inc(ln_eps_ready, 1)
            pool.memset(ident[:], 0.0).then_inc(pool_steps, 1)
            pool.memset(join[:], 1.0).then_inc(pool_steps, 1)
            pool.iota(iota_sb[:], pattern=[[1, WINDOW]], base=0, channel_multiplier=0,
                      allow_small_or_imprecise_dtypes=True).then_inc(consts_ready, 1)
            pool.iota(window_start[:], pattern=[[WINDOW, WINDOWS]], base=0, channel_multiplier=0,
                      allow_small_or_imprecise_dtypes=True).then_inc(consts_ready, 1)
            pool.iota(group_key[:], pattern=[[P, G]], base=-MIDDLE * P, channel_multiplier=1,
                      allow_small_or_imprecise_dtypes=True).then_inc(consts_ready, 1)
            pool.iota(less_group_key[:], pattern=[[-P, G]], base=MIDDLE * P, channel_multiplier=-1,
                      allow_small_or_imprecise_dtypes=True).then_inc(consts_ready, 1)
            pool.memset(one[:], 1.0).then_inc(consts_ready, 1)
            pool.wait_ge(pool_steps, 2)
            pool.affine_select(out=ident[:], in_=ident[:], compare_op=ALU.not_equal, fill=1.0, base=0,
                               pattern=[[-1, P]], channel_multiplier=1).then_inc(consts_ready, 1)
            pool.affine_select(out=join[:], in_=join[:], compare_op=ALU.is_ge, fill=0.0, base=0,
                               pattern=[[-S, F]], channel_multiplier=1).then_inc(pool_steps, 1)
            pool.wait_ge(pool_steps, 3)
            pool.affine_select(out=join[:], in_=join[:], compare_op=ALU.is_ge, fill=0.0, base=S - 1,
                               pattern=[[S, F]], channel_multiplier=-1).then_inc(consts_ready, 1)

            def gather(l, slot, tiles, landed):
                pool.sem_inc(gathers_begun, 1)
                for j in range(tiles):
                    pool.indirect_dma_start(
                        rows[:, slot, j, :], None, tables[l],
                        bass.IndirectOffsetOnAxis(ap=src_i[:, slot, j:j + 1], axis=0),
                    ).then_inc(landed, 16)

            for l in range(LAYERS):
                for k in range(HELPED):
                    if l == 1:
                        pool.wait_ge(product_ready, k + 1)
                        add_product(pool, k).then_inc(x1_ready, 1)
                    pool.wait_ge(mean_ready, l * HELPED + k + 1)
                    center(pool, k).then_inc(centered_ready, 1)

                def step(s, phase, r, left):
                    slot = phase % SLOTS
                    pool.wait_ge(loaded[l][slot], 16 * LOADS[l] * (uses(phase, r) + 1))
                    pool.wait_ge(messages_ready[l], freed(s))
                    pool.wait_ge(table_stored[l], 16 * CHUNKS)
                    gather(l, slot, TILES if whole(s) else GT[phase], gathered[l][slot])
                over_supertiles(pool, step)
                with pool.If(spread_beyond(pool) > 0):
                    with pool.Fori(0, NS) as s:
                        pool.wait_ge(far_loaded[l], 16 * LOADS[l] * (s + 1))
                        gather(l, 0, TILES, far_gathered[l])

        @block.scalar
        def _(act):
            act.wait_ge(ln_eps_ready, 2)
            nc.scalar.activation(root_eps[:], ln_eps[:], ACT.Sqrt)
            act.wait_ge(consts_ready, 7)

            def square(l, k):
                if k < HELPED:
                    act.wait_ge(centered_ready, l * HELPED + k + 1)
                else:
                    act.wait_ge(last_centered, l + 1)
                nc.scalar.activation(squares[k], centered[:, chunk(k), :], ACT.Square).then_inc(squares_ready, 1)

            def table_part1(l, k):
                for g in range(k * GC, (k + 1) * GC):
                    last = nc.scalar.activation(parts_v[:, g, :, :, 0], centered[:, g * J:(g + 1) * J, :], ACT.Copy)
                last.then_inc(part1_ready, 1)

            def deviation(l, k):
                act.wait_ge(var_ready, l * CHUNKS + k + 1)
                nc.scalar.activation(std[:, chunk(k)], sumsq[:, chunk(k)], ACT.Sqrt, bias=ln_eps[0:NP, 0:1],
                                     scale=1.0 / F).then_inc(std_ready, 1)

            def first_part(l, slot, ready):
                nc.scalar.activation(message[:, slot, :, 0], summed(l, slot),
                                     ACT.Copy if l == 0 else ACT.Relu).then_inc(ready, 1)

            def second_part(l, slot, ready):
                nc.scalar.activation(message[:, slot, :, 1], summed(l, slot), ACT.Copy).then_inc(ready, 1)

            for l in range(LAYERS):
                def store_table(k):
                    act.wait_ge(table_ready, l * CHUNKS + k + 1)
                    act.dma_start(tables_v[l][:, chunk(k), :], centered[:, chunk(k), :]).then_inc(table_stored[l], 16)

                for i in range(CHUNKS + 3):
                    if 0 <= i - 2 < CHUNKS:
                        deviation(l, i - 2)
                    if i < CHUNKS:
                        square(l, i)
                    if 0 <= i - 3 < CHUNKS:
                        store_table(i - 3)
                if l == 0:
                    act.dma_start(dst_all, dst_pv).then_inc(dst_loaded, 16)
                for k in range(CHUNKS):
                    table_part1(l, k)

                def src_onehots(n, phase):
                    slot, edges = phase % SLOTS, PT[phase] * P
                    act.wait_ge(key_copied[l], n)
                    for b in range(ACT_BATCHES):
                        groups = range(DVE_GROUPS + b * BATCH, DVE_GROUPS + (b + 1) * BATCH)
                        for g in groups:
                            last = nc.scalar.activation(src_onehot[slot][:, g, 0:edges], key_copy[:, 0:edges], ACT.Abs,
                                                        bias=less_group_key[:, g:g + 1])
                        last.then_inc(distance_ready[l], 1)
                        act.wait_ge(distance_ready[l], (n - 1) * ACT_BATCHES + b + 1)
                        for g in groups:
                            last = nc.scalar.activation(src_onehot[slot][:, g, 0:edges], src_onehot[slot][:, g, 0:edges], ACT.Relu,
                                                        bias=one[0:NP, 0:1], scale=-1.0)
                        last.then_inc(act_onehot_ready[l], 1)

                def copy_window(s):
                    act.wait_ge(agg_ready[l], s + 1)
                    nc.scalar.activation(window_sums[:], agg, ACT.Copy).then_inc(agg_copied[l], 1)

                def step(s, phase, r, left):
                    slot = phase % SLOTS
                    if left >= 2:
                        if not whole(s):
                            act.wait_ge(messages_ready[l], done(s - 1))
                        src_onehots(s + 1, (phase + 1) % ROUND)
                    if not (isinstance(s, int) and s == 0):
                        copy_window(s - 1)
                    if isinstance(s, int) and s == 0:
                        if l == 1:
                            act.wait_ge(nodes_ready, CHUNKS)
                        nc.scalar.activation(acc[:], zero[0:F, 0:1].to_broadcast([F, ACC]), ACT.Copy).then_inc(acc_zeroed, 1)
                        act.wait_ge(parts_ready, (l + 1) * CHUNKS)
                    if l == 0:
                        act.wait_ge(gathered[l][slot], gathers(s, phase, r))
                        if not whole(s):
                            act.wait_ge(rows_ready[l], s)
                    else:
                        act.wait_ge(rows_added, s + 1)
                    first_part(l, slot, message1_ready[l])
                    act.wait_ge(message1_left[l], s + 1)
                    second_part(l, slot, message2_ready[l])
                over_supertiles(act, step)
                copy_window(NS - 1)
                with act.If(spread_beyond(act) > 0):
                    with act.Fori(0, NS) as s:
                        if l == 0:
                            act.wait_ge(far_gathered[l], 16 * TILES * (s + 1))
                        else:
                            act.wait_ge(far_added_rows, s + 1)
                        first_part(l, 0, far_message1[l])
                        act.wait_ge(far_left[l], s + 1)
                        second_part(l, 0, far_message2[l])

            for k in range(CHUNKS):
                act.wait_ge(result_ready, k + 1)
                act.dma_start(out_v[:, chunk(k), :], xs[:, chunk(k), :]).then_inc(out_stored, 16)
            act.wait_ge(out_stored, 16 * CHUNKS)

        @block.tensor
        def _(pe):
            def search_windows():
                pe.wait_ge(ends_ready, 2)
                for k, turned in enumerate((low_ps, high_ps)):
                    nc.tensor.transpose(turned, ends[:, k, :], ident[:]).then_inc(ends_turned, 1)
                pe.wait_ge(spread_ready, 2)
                for k in range(2):
                    nc.tensor.matmul(spread_ps[k], spread[:, k, :], ident[0:NS, 0:NS], start=True,
                                     stop=True).then_inc(base_spread, 1)

            def products(slot, finished):
                for j in range(TILES):
                    last = nc.tensor.matmul(agg, message[:, slot, j * F:(j + 1) * F, :].rearrange("p f s -> p (f s)"),
                                            dst_onehot[:, slot, j, :], start=(j == 0), stop=(j == TILES - 1))
                last.then_inc(finished, 1)

            for l in range(LAYERS):
                def keys(n, phase):
                    slot = phase % SLOTS
                    for t in range(PT[phase]):
                        column = src_key[:, bass.ds(n * PTMAX + PTMAX - PT[phase] + t, 1)].to_broadcast([P, NP])
                        last = nc.tensor.transpose(key_rows[slot][:, t * P:(t + 1) * P], column, ident16[:])
                    last.then_inc(key_rows_ready[l], 1)

                def join_window(s):
                    pe.wait_ge(agg_copied[l], s + 1)
                    nc.tensor.matmul(joined, join[:], window_sums[:], start=True, stop=True).then_inc(joined_ready[l], 1)

                def candidate_rows(n, phase, joins, more):
                    for t in range(PT[phase]):
                        if joins and t == 0:
                            pe.wait_ge(early_picked[l], n - 1)
                        if joins and t == EARLY:
                            pe.wait_ge(late_picked[l], n - 1)
                        for g in range(G):
                            if not joins and t == 0 and g % GC == 0:
                                pe.wait_ge(parts_ready, l * CHUNKS + g // GC + 1)
                            if t == 0 and g % BATCH == 0 and g < DVE_GROUPS:
                                pe.wait_ge(src_onehot_ready[l], (n - 1) * DVE_BATCHES + g // BATCH + 1)
                            elif t == 0 and g % BATCH == 0:
                                pe.wait_ge(act_onehot_ready[l], (n - 1) * ACT_BATCHES + g // BATCH - DVE_BATCHES + 1)
                            last = nc.tensor.matmul(candidates[:, t, 0:WIDE],
                                                    src_onehot[phase % SLOTS][:, g, t * P:(t + 1) * P],
                                                    parts[:, g * WIDE:(g + 1) * WIDE], start=(g == 0), stop=(g == G - 1))
                        if t == EARLY - 1:
                            last.then_inc(early_candidates[l], 1)
                        if t == PT[phase] - 2 and not joins and l == 0:
                            search_windows()
                        if t == 0 and joins:
                            join_window(n - 2)
                        if t == 0 and more:
                            keys(n + 2, (phase + 2) % ROUND)
                    last.then_inc(late_candidates[l], 1)

                pe.wait_ge(src_key_ready, 2)
                if l == 1:
                    pe.wait_ge(product_ready, CHUNKS)
                keys(1, 1)
                keys(2, 2)

                def step(s, phase, r, left):
                    slot = phase % SLOTS
                    first = isinstance(s, int) and s == 0
                    if left >= 2:
                        candidate_rows(s + 1, (phase + 1) % ROUND, not first, left == 4)
                    else:
                        join_window(s - 1)
                    pe.wait_ge(messages_ready[l], done(s))
                    products(slot, agg_ready[l])
                over_supertiles(pe, step)
                join_window(NS - 1)
                with pe.If(spread_beyond(pe) > 0):
                    with pe.Fori(0, NS) as s:
                        with pe.Fori(0, WINDOWS) as w:
                            pe.wait_ge(far_messages[l], s + 1)
                            pe.wait_ge(far_onehot[l], s * WINDOWS + w + 1)
                            pe.wait_ge(far_added[l], s * WINDOWS + w + 1)
                            products(0, far_agg[l])
                            pe.wait_ge(far_copied[l], s * WINDOWS + w + 1)
                            nc.tensor.matmul(joined, join[:], window_sums[:], start=True, stop=True).then_inc(far_joined[l], 1)
                pe.wait_ge(acc_final, l + 1)
                for k in range(CHUNKS):
                    if k > 1:
                        pe.wait_ge(product_ready if l == 0 else nodes_used, k - 1)
                    for c in range(CC):
                        node = k * CC + c
                        last = nc.tensor.transpose(nodes_in(k)[:, c, :], acc[:, node:node + C * (NP - 1) + 1:C],
                                                   ident[0:F, 0:F])
                    last.then_inc(nodes_ready, 1)

        @block.vector
        def _(dve):
            steps = [0]

            def link(ins):
                steps[0] += 1
                ins.then_inc(dve_steps, 1)
                dve.wait_ge(dve_steps, steps[0])

            def mean_of(l, k):
                link(nc.vector.reduce_sum(sums[:, chunk(k)], xs[:, chunk(k), :], AX))
                last = nc.vector.tensor_scalar(mean[:, chunk(k)], sums[:, chunk(k)], 1.0 / F, None, ALU.mult)
                if k < HELPED:
                    last.then_inc(mean_ready, 1)
                else:
                    link(last)
                    center(nc.vector, k).then_inc(last_centered, 1)

            def sum_squares(l, k):
                dve.wait_ge(squares_ready, l * CHUNKS + k + 1)
                nc.vector.reduce_sum(sumsq[:, chunk(k)], squares[k], AX).then_inc(var_ready, 1)

            def table_rows(l, k):
                dve.wait_ge(std_ready, l * CHUNKS + k + 1)
                link(nc.vector.reciprocal(rstd[:, chunk(k)], std[:, chunk(k)]))
                if l == 0:
                    link(nc.vector.tensor_tensor(rstd[:, chunk(k)], rstd[:, chunk(k)], cj[:, chunk(k)], ALU.mult))
                nc.vector.scalar_tensor_tensor(centered[:, chunk(k), :], centered[:, chunk(k), :], 0.0,
                                               per_node(rstd, k), ALU.max, ALU.mult).then_inc(table_ready, 1)

            def table_parts(l, k):
                dve.wait_ge(table_ready, l * CHUNKS + k + 1)
                dve.wait_ge(part1_ready, l * CHUNKS + k + 1)
                part = [parts_v[:, k * GC:(k + 1) * GC, :, :, i] for i in range(S)]
                whole = centered[:, chunk(k), :].rearrange("p (g j) f -> p g j f", j=J)
                left = left_over[k % len(left_over)]
                link(nc.vector.tensor_tensor(left, whole, part[0], ALU.subtract))
                link(nc.vector.tensor_copy(part[1], left))
                nc.vector.tensor_tensor(part[2], left, part[1], ALU.subtract).then_inc(parts_ready, 1)
                dve.wait_ge(parts_ready, l * CHUNKS + k + 1)

            for l in range(LAYERS):
                dve.sem_inc(messages_ready[l], SLOTS)

            for i in range(CHUNKS + 3):
                if i < CHUNKS:
                    dve.wait_ge(x_loaded[i], 16)
                    mean_of(0, i)
                if 0 <= i - 2 < CHUNKS:
                    sum_squares(0, i - 2)
                if 0 <= i - 3 < CHUNKS:
                    if i == 3:
                        dve.wait_ge(small_loaded, 48)
                    table_rows(0, i - 3)
            link(nc.vector.tensor_scalar(eps1[:], eps_in[:], 1.0, None, ALU.add))

            dve.wait_ge(consts_ready, 7)
            nc.vector.tensor_copy(ident16[:], ident[:]).then_inc(src_key_ready, 1)
            link(nc.vector.tensor_copy(iota, iota_sb[:]))
            dve.wait_ge(src_pe_loaded, 16)
            src_flat = src_pe.rearrange("p s t -> p (s t)")
            link(nc.vector.tensor_scalar(scaled, src_flat, 1.0 / C, 0.5 / C - 0.5, ALU.mult, ALU.add))
            link(nc.vector.tensor_scalar(row_of, scaled, TO_INTEGER, TO_INTEGER, ALU.add, ALU.subtract))
            link(nc.vector.scalar_tensor_tensor(col_of, row_of, -float(C), src_flat, ALU.mult, ALU.add))
            link(nc.vector.tensor_scalar(scaled, col_of, 1.0 / J, 0.5 / J - 0.5, ALU.mult, ALU.add))
            link(nc.vector.tensor_scalar(group_of, scaled, TO_INTEGER, TO_INTEGER, ALU.add, ALU.subtract))
            link(nc.vector.scalar_tensor_tensor(member_of[:], group_of, -float(J), col_of, ALU.mult, ALU.add))
            link(nc.vector.tensor_scalar(group_of, group_of, float(P), -float(MIDDLE * P), ALU.mult, ALU.add))
            nc.vector.tensor_tensor(src_key[:], group_of, row_of, ALU.add).then_inc(src_key_ready, 1)

            def search_windows():
                dve.wait_ge(dst_loaded, 16)
                nc.vector.tensor_reduce(ends[:, 0, :], dst_all, AX, ALU.min).then_inc(ends_ready, 1)
                nc.vector.tensor_reduce(ends[:, 1, :], dst_all, AX, ALU.max).then_inc(ends_ready, 1)
                dve.wait_ge(ends_turned, 2)
                link(nc.vector.tensor_reduce(ends_of[:, 0:1], low_ps, AX, ALU.min))
                link(nc.vector.tensor_reduce(ends_of[:, 1:2], high_ps, AX, ALU.max))
                link(nc.vector.tensor_tensor(span, ends_of[:, 1:2], ends_of[:, 0:1], ALU.subtract))
                link(nc.vector.tensor_scalar(beyond, span, float(WINDOW), None, ALU.is_ge))
                nc.vector.tensor_copy(spread[:, 0, :], ends_of[:, 0:1].to_broadcast([NS, P])).then_inc(spread_ready, 1)
                nc.vector.tensor_copy(spread[:, 1, :], beyond.to_broadcast([NS, P])).then_inc(spread_ready, 1)

            def place_windows():
                dve.wait_ge(base_spread, 2)
                link(nc.vector.tensor_copy(base[:], spread_ps[0]))
                link(nc.vector.tensor_copy(base_i[:], spread_ps[0]))
                link(nc.vector.reduce_max(any_beyond[:], spread_ps[1], AX))
                nc.vector.tensor_copy(any_beyond_i[:], any_beyond[:]).then_inc(flag_ready, 1)
                link(nc.vector.tensor_scalar(base1[:], base[:], 1.0, None, ALU.add))

            def window_keys(some):
                n = len(range(NS)[some])
                link(nc.vector.tensor_tensor(key[:, some, :], dst_all[:, some, :],
                                             base[:, some].unsqueeze(2).to_broadcast([P, n, TILES]), ALU.subtract))

            for l in range(LAYERS):
                def src_onehots(n, phase):
                    slot, edges = phase % SLOTS, PT[phase] * P
                    dve.wait_ge(key_rows_ready[l], n)
                    if not isinstance(n, int):
                        dve.wait_ge(distance_ready[l], (n - 1) * ACT_BATCHES)
                    nc.vector.tensor_copy(key_copy[:, 0:edges], key_rows[slot][:, 0:edges]).then_inc(key_copied[l], 1)
                    for g in range(DVE_GROUPS):
                        one = nc.vector.tensor_scalar(src_onehot[slot][:, g, 0:edges], key_rows[slot][:, 0:edges],
                                                      group_key[:, g:g + 1], None, ALU.is_equal)
                        if g % BATCH == BATCH - 1:
                            one.then_inc(src_onehot_ready[l], 1)

                def dst_onehots(slot, keys):
                    return nc.vector.tensor_tensor(
                        dst_onehot[:, slot, :, :], iota.unsqueeze(1).to_broadcast([P, TILES, WINDOW]),
                        keys.unsqueeze(2).to_broadcast([P, TILES, WINDOW]), ALU.is_equal)

                def add_rows(slot, added):
                    nc.vector.tensor_tensor(attr[:, slot, :, :], attr[:, slot, :, :], rows[:, slot, :, :],
                                            ALU.add).then_inc(added, 1)

                def after_first_part(slot, ready):
                    if l == 0:
                        nc.vector.tensor_tensor(summed(l, slot), summed(l, slot), message[:, slot, :, 0],
                                                ALU.subtract).then_inc(ready, 1)
                    else:
                        nc.vector.scalar_tensor_tensor(summed(l, slot), summed(l, slot), 0.0, message[:, slot, :, 0],
                                                       ALU.max, ALU.subtract).then_inc(ready, 1)

                def third_part(slot, ready):
                    nc.vector.tensor_tensor(message[:, slot, :, 2], summed(l, slot), message[:, slot, :, 1],
                                            ALU.subtract).then_inc(ready, 1)

                def add_window(s):
                    first = dve.value_load(base_i[0:1, bass.ds(s, 1)], min_val=0, max_val=N - 1)
                    dve.wait_ge(joined_ready[l], s + 1)
                    dve.wait_ge(acc_added[l], s + 1)
                    window = acc[:, bass.ds(first, WINDOW)]
                    nc.vector.tensor_tensor(window, window, joined, ALU.add).then_inc(acc_added[l], 1)

                table_parts(l, 0)
                src_onehots(1, 1)
                for k in range(1, CHUNKS):
                    table_parts(l, k)
                if l == 0:
                    search_windows()
                    place_windows()
                    window_keys(slice(0, 1))

                def step(s, phase, r, left):
                    slot = phase % SLOTS
                    first = isinstance(s, int) and s == 0
                    if left >= 2 and not first:
                        src_onehots(s + 1, (phase + 1) % ROUND)
                    if first:
                        dve.wait_ge(key_rows_ready[l], 3)
                    elif slot == 1 and left > 2:
                        dve.wait_ge(key_rows_ready[l], s + 2)
                    dst_onehots(slot, key[:, bass.ds(s, 1), :].rearrange("p o j -> p (o j)"))
                    if not whole(s):
                        n = PT[phase]

                        def pick(first, end):
                            tiles = slice(first, end)
                            return nc.vector.tensor_tensor(
                                picked[:, first * WIDE:end * WIDE].rearrange("p (t q j) -> p t q j", t=end - first, j=J),
                                candidates[:, tiles, 0:WIDE].rearrange("p t (q j) -> p t q j", j=J),
                                member[:, tiles, :].unsqueeze(2).to_broadcast([P, end - first, F * S, J]), ALU.mult)

                        nc.vector.tensor_tensor(
                            member[:, 0:n, :], iota_sb[:, 0:J].unsqueeze(1).to_broadcast([P, n, J]),
                            member_of[:, bass.ds(s * PTMAX + PTMAX - n, n)].unsqueeze(2).to_broadcast([P, n, J]),
                            ALU.is_equal).then_inc(member_ready[l], 1)
                        dve.wait_ge(member_ready[l], s)
                        dve.wait_ge(early_candidates[l], s)
                        pick(0, EARLY).then_inc(early_picked[l], 1)
                        dve.wait_ge(late_candidates[l], s)
                        pick(EARLY, n).then_inc(late_picked[l], 1)
                        dve.wait_ge(early_picked[l], s)
                        dve.wait_ge(late_picked[l], s)
                        nc.vector.reduce_sum(rows[:, slot, GT[phase]:TILES, :],
                                             picked[:, 0:n * WIDE].rearrange("p (t f k) -> p t f k", t=n, f=F),
                                             AX).then_inc(rows_ready[l], 1)
                    if l == 1:
                        if not whole(s):
                            dve.wait_ge(rows_ready[l], s)
                        dve.wait_ge(gathered[l][slot], gathers(s, phase, r))
                        dve.wait_ge(loaded[l][slot], 16 * LOADS[l] * (uses(phase, r) + 1))
                        add_rows(slot, rows_added)
                    dve.wait_ge(message1_ready[l], s + 1)
                    after_first_part(slot, message1_left[l])
                    if not first:
                        add_window(s - 1)
                    dve.wait_ge(message2_ready[l], s + 1)
                    third_part(slot, messages_ready[l])
                    if first:
                        dve.wait_ge(acc_zeroed, l + 1)
                        dve.sem_inc(acc_added[l], 1)
                    if first and l == 0:
                        window_keys(slice(1, NS))
                    elif first:
                        link(nc.vector.scalar_tensor_tensor(xs[:], centered[:], eps1[:, 0:1], xs[:], ALU.mult, ALU.add))
                over_supertiles(dve, step)
                add_window(NS - 1)
                dve.wait_ge(acc_added[l], NS + 1)

                with dve.If(spread_beyond(dve) > 0):
                    dve.sem_inc(far_added[l], 1)
                    with dve.Fori(0, NS) as s:
                        dve.wait_ge(far_gathered[l], 16 * TILES * (s + 1))
                        if l == 1:
                            add_rows(0, far_added_rows)
                        keys = key[:, bass.ds(s, 1), :].rearrange("p o j -> p (o j)")
                        nc.vector.tensor_scalar(far, keys, float(WINDOW), None, ALU.is_ge).then_inc(far_steps[l], 1)
                        dve.wait_ge(far_steps[l], 2 * s + 1)
                        nc.vector.scalar_tensor_tensor(far_dst, keys, base1[:, bass.ds(s, 1)], far, ALU.add,
                                                       ALU.mult).then_inc(far_steps[l], 1)
                        dve.wait_ge(far_message1[l], s + 1)
                        after_first_part(0, far_left[l])
                        dve.wait_ge(far_message2[l], s + 1)
                        third_part(0, far_messages[l])
                        with dve.Fori(0, WINDOWS) as w:
                            nth = s * WINDOWS + w + 1
                            dve.wait_ge(far_steps[l], 2 * s + 2)
                            nc.vector.tensor_scalar(far_key, far_dst, window_start[:, bass.ds(w, 1)], 1.0,
                                                    ALU.subtract, ALU.subtract).then_inc(far_key_ready[l], 1)
                            dve.wait_ge(far_key_ready[l], nth)
                            dst_onehots(0, far_key).then_inc(far_onehot[l], 1)
                            dve.wait_ge(far_agg[l], nth)
                            nc.vector.tensor_copy(window_sums[:], agg).then_inc(far_copied[l], 1)
                            dve.wait_ge(far_joined[l], nth)
                            dve.wait_ge(far_added[l], nth)
                            window = acc[:, bass.ds(w * WINDOW, WINDOW)]
                            nc.vector.tensor_tensor(window, window, joined, ALU.add).then_inc(far_added[l], 1)
                    dve.wait_ge(far_added[l], NS * WINDOWS + 1)
                dve.sem_inc(acc_final, 1)

                def read_nodes(k):
                    dve.wait_ge(nodes_ready, l * CHUNKS + k + 1)

                if l == 0:
                    dve.wait_ge(table_stored[0], 16 * CHUNKS)
                    for i in range(CHUNKS + 3):
                        if i < CHUNKS:
                            read_nodes(i)
                            nc.vector.tensor_tensor(product[i], nodes_in(i), per_node(ci, i), ALU.mult).then_inc(product_ready, 1)
                        if 0 <= i - 2 < CHUNKS:
                            sum_squares(1, i - 2)
                        if 0 <= i - 1 < HELPED:
                            dve.wait_ge(x1_ready, i)
                            mean_of(1, i - 1)
                        if i == HELPED:
                            dve.wait_ge(product_ready, CHUNKS)
                            link(add_product(nc.vector, HELPED))
                            mean_of(1, HELPED)
                        if 0 <= i - 3 < CHUNKS:
                            table_rows(1, i - 3)
                else:
                    for k in range(CHUNKS):
                        read_nodes(k)
                        nc.vector.tensor_tensor(xs[:, chunk(k), :], xs[:, chunk(k), :], nodes_in(k),
                                                ALU.add).then_inc(nodes_used, 1)
                        dve.wait_ge(nodes_used, k + 1)
                        dve.sem_inc(result_ready, 1)


_INS = ['x', 'src', 'dst', 'edge_attr_32', 'node_vec1', 'node_vec1_n2', 'L1_gnn_eps']


def kernel(**inputs):
    import numpy as np
    import concourse.bacc as bacc
    from concourse.bass_utils import run_bass_kernel_spmd

    nc = bacc.Bacc("TRN2", target_bir_lowering=False, num_devices=1)
    arrays, args = {}, []
    for name in _INS:
        a = np.ascontiguousarray(inputs[name])
        arrays[f"in_{name}"] = a
        args.append(nc.dram_tensor(f"in_{name}", a.shape, mybir.dt.from_np(a.dtype), kind="ExternalInput").ap())
    out = nc.dram_tensor("out", inputs['x'].shape, F32, kind="ExternalOutput").ap()
    gnn_two_layers(nc, *args, out)
    r = run_bass_kernel_spmd(nc, [arrays], core_ids=[0])
    return r.results[0]["out"]
```
